# Optimizing a Trainium2 kernel written in Bass

```python
import numpy as np
import jax
import jax.numpy as jnp

def _softmax(x, axis=-1):
    return jax.nn.softmax(x, axis=axis)

def _gelu(x):
    return jax.nn.gelu(x, approximate=True)

def _silu(x):
    return jax.nn.silu(x)

def _sigmoid(x):
    return jax.nn.sigmoid(x)

def _layernorm(x, axis=-1, eps=1e-05):
    m = jnp.mean(x, axis=axis, keepdims=True)
    v = jnp.var(x, axis=axis, keepdims=True)
    return (x - m) / jnp.sqrt(v + eps)

def _scatter_add(tgt, idx, src, axis=0):
    return tgt.at[idx].add(src)

def _segment_sum(src, seg, n):
    return jax.ops.segment_sum(src, seg, n)
kernel_name = 'mk_gnn_preln_d4_gnn_r32_38ebb2'

def setup_inputs(seed: int=0):
    np.random.seed(seed)
    _w = jnp.asarray

    def _rec_inputs():
        import jax
        import jax.numpy as jnp
        _gk = jax.random.key(seed)
        x = -0.0003713 + 1 * jax.random.normal(jax.random.fold_in(_gk, 1), (50000, 128), jnp.float32)
        src = jax.random.randint(jax.random.fold_in(_gk, 2), (50000,), 0, 50000, jnp.int32)
        dst = jax.random.randint(jax.random.fold_in(_gk, 3), (50000,), 0, 50000, jnp.int32)
        _o = jnp.argsort(dst, stable=True)
        src = src[_o]
        dst = dst[_o]
        edge_attr_128 = -5.16925e-05 + 1.00005 * jax.random.normal(jax.random.fold_in(_gk, 12), (50000, 128), jnp.float32)
        edge_attr_64 = -8.16379e-05 + 0.999858 * jax.random.normal(jax.random.fold_in(_gk, 13), (50000, 64), jnp.float32)
        edge_weight = jax.random.uniform(jax.random.fold_in(_gk, 15), (50000,), jnp.float32, 0.0, 1)
        return (x, src, dst, edge_attr_128, edge_attr_64, edge_weight)
    x, src, dst, edge_attr_128, edge_attr_64, edge_weight = _rec_inputs()

    def _L0_gnn_setup():
        import jax, jax.numpy as jnp
        import numpy as np
        N = 3125
        R = 8
        HFR = 128
        HTO = 128
        NNZ = 50000
        key = jax.random.key(seed)
        k1, k2, k3, k4, k5 = jax.random.split(key, 5)
        nodes = jax.random.normal(k1, (N, HFR), dtype=jnp.float32)
        rows = jax.random.randint(k2, (NNZ,), 0, N * R)
        cols = jax.random.randint(k3, (NNZ,), 0, N)
        indices = jnp.stack([rows, cols]).astype(jnp.int64)
        values = jax.random.uniform(k4, (NNZ,), dtype=jnp.float32)
        weights = jax.random.normal(k5, (R, HFR, HTO), dtype=jnp.float32) * np.float32(1.0 / np.sqrt(HFR))
        return {'nodes': nodes, 'indices': indices, 'values': values, 'weights': weights}
    _L0_gnn_all = _L0_gnn_setup()
    _L0_gnn_in = {k: v for k, v in _L0_gnn_all.items() if k in ('weights',)}
    del _L0_gnn_all

    def _L1_gnn_setup():
        import jax, jax.numpy as jnp
        import numpy as np
        N_NODES = 50000
        N_EDGES = 25000
        D = 128

        def _layer_norm(h, gamma, beta, eps=1e-05):
            mu = jnp.mean(h, axis=-1, keepdims=True)
            var = jnp.mean(jnp.square(h - mu), axis=-1, keepdims=True)
            return (h - mu) * jax.lax.rsqrt(var + eps) * gamma + beta
        key = jax.random.key(seed)
        ks = jax.random.split(key, 6)
        s1 = 1.0 / np.sqrt(2 * D)
        s2 = 1.0 / np.sqrt(2 * D)
        return {'x': jax.random.normal(ks[0], (N_NODES, D), dtype=jnp.float32), 'edge_index': jax.random.randint(ks[1], (2, N_EDGES), 0, N_NODES, dtype=jnp.int32), 'edge_attr': jax.random.normal(ks[2], (N_EDGES, D), dtype=jnp.float32), 'W1': jax.random.normal(ks[3], (2 * D, 2 * D), dtype=jnp.float32) * s1, 'b1': jnp.zeros((2 * D,), dtype=jnp.float32), 'W2': jax.random.normal(ks[4], (2 * D, D), dtype=jnp.float32) * s2, 'b2': jnp.zeros((D,), dtype=jnp.float32), 'ln_gamma': jnp.ones((D,), dtype=jnp.float32), 'ln_beta': jnp.zeros((D,), dtype=jnp.float32)}
    _L1_gnn_all = _L1_gnn_setup()
    _L1_gnn_in = {k: v for k, v in _L1_gnn_all.items() if k in ('W1', 'b1', 'W2', 'b2', 'ln_gamma', 'ln_beta')}
    del _L1_gnn_all

    def _L2_gnn_setup():
        import jax, jax.numpy as jnp
        import numpy as np
        N_NODES = 3125
        N_EDGES = 50000
        NDIM_IN = 128
        EDIMS = 64
        NDIM_OUT = 128
        NUM_HEADS = 4
        HEAD_DIM = NDIM_OUT // NUM_HEADS
        key = jax.random.key(seed)
        ks = jax.random.split(key, 10)
        in_dim = NDIM_IN + EDIMS
        b1 = float(np.sqrt(6.0 / (in_dim + NDIM_OUT)))
        b2 = float(np.sqrt(6.0 / (NDIM_OUT + NDIM_OUT)))
        bav = float(np.sqrt(6.0 / (NUM_HEADS + HEAD_DIM)))
        return {'nfeats': jax.random.normal(ks[0], (N_NODES, NDIM_IN), dtype=jnp.float32), 'efeats': jax.random.normal(ks[1], (N_EDGES, EDIMS), dtype=jnp.float32), 'src': jax.random.randint(ks[2], (N_EDGES,), 0, N_NODES, dtype=jnp.int32), 'dst': jax.random.randint(ks[3], (N_EDGES,), 0, N_NODES, dtype=jnp.int32), 'W_proj_w': jax.random.uniform(ks[4], (NDIM_OUT, in_dim), jnp.float32, -b1, b1), 'W_proj_b': jnp.zeros((NDIM_OUT,), jnp.float32), 'attn_vec': jax.random.uniform(ks[5], (NUM_HEADS, HEAD_DIM), jnp.float32, -bav, bav), 'W_out_w': jax.random.uniform(ks[6], (NDIM_OUT, NDIM_OUT), jnp.float32, -b2, b2), 'W_out_b': jnp.zeros((NDIM_OUT,), jnp.float32), 'ln_gamma': jnp.ones((NDIM_OUT,), jnp.float32), 'ln_beta': jnp.zeros((NDIM_OUT,), jnp.float32)}
    _L2_gnn_all = _L2_gnn_setup()
    _L2_gnn_in = {k: v for k, v in _L2_gnn_all.items() if k in ('W_proj_w', 'W_proj_b', 'attn_vec', 'W_out_w', 'W_out_b', 'ln_gamma', 'ln_beta')}
    del _L2_gnn_all

    def _L3_gnn_setup():
        import jax, jax.numpy as jnp
        import numpy as np
        N_NODES = 50000
        N_EDGES = 25000
        F_IN = 128
        HIDDEN = 256
        F_OUT = 128

        def _glorot(key, shape):
            fan_in, fan_out = shape
            lim = jnp.sqrt(6.0 / (fan_in + fan_out))
            return jax.random.uniform(key, shape, jnp.float32, -lim, lim)

        def _sage_conv(x, src, dst, W_l, b, W_r, n_nodes):
            agg = jax.ops.segment_sum(x[src], dst, num_segments=n_nodes)
            cnt = jax.ops.segment_sum(jnp.ones((src.shape[0],), x.dtype), dst, num_segments=n_nodes)
            mean = agg / jnp.maximum(cnt, 1.0)[:, None]
            return mean @ W_l + b + x @ W_r
        key = jax.random.key(seed)
        ks = jax.random.split(key, 8)
        x = jax.random.normal(ks[0], (N_NODES, F_IN), jnp.float32)
        edge_index = jax.random.randint(ks[1], (2, N_EDGES), 0, N_NODES, jnp.int64)
        return {'x': x, 'edge_index': edge_index, 'W1_l': _glorot(ks[2], (F_IN, HIDDEN)), 'b1': jnp.zeros((HIDDEN,), jnp.float32), 'W1_r': _glorot(ks[3], (F_IN, HIDDEN)), 'W2_l': _glorot(ks[4], (HIDDEN, F_OUT)), 'b2': jnp.zeros((F_OUT,), jnp.float32), 'W2_r': _glorot(ks[5], (HIDDEN, F_OUT))}
    _L3_gnn_all = _L3_gnn_setup()
    _L3_gnn_in = {k: v for k, v in _L3_gnn_all.items() if k in ('W1_l', 'b1', 'W1_r', 'W2_l', 'b2', 'W2_r')}
    del _L3_gnn_all
    return {'x': x, 'src': src, 'dst': dst, 'edge_attr_128': edge_attr_128, 'edge_attr_64': edge_attr_64, 'edge_weight': edge_weight, 'L0_gnn_weights': _L0_gnn_in['weights'], 'L1_gnn_W1': _L1_gnn_in['W1'], 'L1_gnn_b1': _L1_gnn_in['b1'], 'L1_gnn_W2': _L1_gnn_in['W2'], 'L1_gnn_b2': _L1_gnn_in['b2'], 'L1_gnn_ln_gamma': _L1_gnn_in['ln_gamma'], 'L1_gnn_ln_beta': _L1_gnn_in['ln_beta'], 'L2_gnn_W_proj_w': _L2_gnn_in['W_proj_w'], 'L2_gnn_W_proj_b': _L2_gnn_in['W_proj_b'], 'L2_gnn_attn_vec': _L2_gnn_in['attn_vec'], 'L2_gnn_W_out_w': _L2_gnn_in['W_out_w'], 'L2_gnn_W_out_b': _L2_gnn_in['W_out_b'], 'L2_gnn_ln_gamma': _L2_gnn_in['ln_gamma'], 'L2_gnn_ln_beta': _L2_gnn_in['ln_beta'], 'L3_gnn_W1_l': _L3_gnn_in['W1_l'], 'L3_gnn_b1': _L3_gnn_in['b1'], 'L3_gnn_W1_r': _L3_gnn_in['W1_r'], 'L3_gnn_W2_l': _L3_gnn_in['W2_l'], 'L3_gnn_b2': _L3_gnn_in['b2'], 'L3_gnn_W2_r': _L3_gnn_in['W2_r']}

def reference(x, src, dst, edge_attr_128, edge_attr_64, edge_weight, L0_gnn_weights, L1_gnn_W1, L1_gnn_b1, L1_gnn_W2, L1_gnn_b2, L1_gnn_ln_gamma, L1_gnn_ln_beta, L2_gnn_W_proj_w, L2_gnn_W_proj_b, L2_gnn_attn_vec, L2_gnn_W_out_w, L2_gnn_W_out_b, L2_gnn_ln_gamma, L2_gnn_ln_beta, L3_gnn_W1_l, L3_gnn_b1, L3_gnn_W1_r, L3_gnn_W2_l, L3_gnn_b2, L3_gnn_W2_r):
    import jax
    import jax.numpy as jnp

    def _L0_gnn_ref(nodes, indices, values, weights):
        import jax, jax.numpy as jnp
        import numpy as np
        N = 3125
        R = 8
        HFR = 128
        HTO = 128
        NNZ = 50000
        n = nodes.shape[0]
        r = weights.shape[0]
        rows, cols = (indices[0], indices[1])
        msgs = values[:, None] * nodes[cols]
        agg = jax.ops.segment_sum(msgs, rows, num_segments=n * r)
        agg = agg.reshape(r, n, -1)
        out = jnp.einsum('rij,rnj->ni', weights, agg)
        return jax.nn.relu(out)

    def _L1_gnn_ref(x, edge_index, edge_attr, W1, b1, W2, b2, ln_gamma, ln_beta):
        import jax, jax.numpy as jnp
        import numpy as np
        N_NODES = 50000
        N_EDGES = 25000
        D = 128

        def _layer_norm(h, gamma, beta, eps=1e-05):
            mu = jnp.mean(h, axis=-1, keepdims=True)
            var = jnp.mean(jnp.square(h - mu), axis=-1, keepdims=True)
            return (h - mu) * jax.lax.rsqrt(var + eps) * gamma + beta
        j = edge_index[1]
        agg = jax.ops.segment_sum(edge_attr, j, num_segments=x.shape[0])
        out = jnp.concatenate([x, agg], axis=-1)
        h = jax.nn.silu(out @ W1 + b1)
        h = h @ W2 + b2
        h = _layer_norm(h, ln_gamma, ln_beta)
        return x + h

    def _L2_gnn_ref(nfeats, efeats, src, dst, W_proj_w, W_proj_b, attn_vec, W_out_w, W_out_b, ln_gamma, ln_beta):
        import jax, jax.numpy as jnp
        import numpy as np
        N_NODES = 3125
        N_EDGES = 50000
        NDIM_IN = 128
        EDIMS = 64
        NDIM_OUT = 128
        NUM_HEADS = 4
        HEAD_DIM = NDIM_OUT // NUM_HEADS
        N = nfeats.shape[0]
        H, D = attn_vec.shape
        x = jnp.concatenate([nfeats[src], efeats], axis=1)
        x_proj = (x @ W_proj_w.T + W_proj_b).reshape(-1, H, D)
        e = jnp.sum(x_proj * attn_vec, axis=-1)
        emax = jax.ops.segment_max(e, dst, num_segments=N)
        ex = jnp.exp(e - emax[dst])
        denom = jax.ops.segment_sum(ex, dst, num_segments=N)
        alpha = ex / denom[dst]
        m = (x_proj * alpha[:, :, None]).reshape(-1, H * D)
        h_neigh = jax.ops.segment_sum(m, dst, num_segments=N)
        h = jax.nn.relu((h_neigh + nfeats) @ W_out_w.T + W_out_b)
        mu = jnp.mean(h, axis=-1, keepdims=True)
        var = jnp.mean((h - mu) ** 2, axis=-1, keepdims=True)
        return (h - mu) * jax.lax.rsqrt(var + 1e-05) * ln_gamma + ln_beta

    def _L3_gnn_ref(x, edge_index, W1_l, b1, W1_r, W2_l, b2, W2_r):
        import jax, jax.numpy as jnp
        import numpy as np
        N_NODES = 50000
        N_EDGES = 25000
        F_IN = 128
        HIDDEN = 256
        F_OUT = 128

        def _glorot(key, shape):
            fan_in, fan_out = shape
            lim = jnp.sqrt(6.0 / (fan_in + fan_out))
            return jax.random.uniform(key, shape, jnp.float32, -lim, lim)

        def _sage_conv(x, src, dst, W_l, b, W_r, n_nodes):
            agg = jax.ops.segment_sum(x[src], dst, num_segments=n_nodes)
            cnt = jax.ops.segment_sum(jnp.ones((src.shape[0],), x.dtype), dst, num_segments=n_nodes)
            mean = agg / jnp.maximum(cnt, 1.0)[:, None]
            return mean @ W_l + b + x @ W_r
        src, dst = (edge_index[0], edge_index[1])
        n = x.shape[0]
        h = _sage_conv(x, src, dst, W1_l, b1, W1_r, n)
        h = jax.nn.relu(h)
        out = _sage_conv(h, src, dst, W2_l, b2, W2_r, n)
        return out
    edge_index = jnp.stack([src, dst])
    h = jnp.maximum(_layernorm(x, axis=-1), 0.0)
    x = x + _L0_gnn_ref(h, edge_index, edge_weight, L0_gnn_weights)
    h = jnp.maximum(_layernorm(x, axis=-1), 0.0)
    x = x + _L1_gnn_ref(h, edge_index, edge_attr_128, L1_gnn_W1, L1_gnn_b1, L1_gnn_W2, L1_gnn_b2, L1_gnn_ln_gamma, L1_gnn_ln_beta)
    h = jnp.maximum(_layernorm(x, axis=-1), 0.0)
    x = x + _L2_gnn_ref(h, edge_attr_64, src, dst, L2_gnn_W_proj_w, L2_gnn_W_proj_b, L2_gnn_attn_vec, L2_gnn_W_out_w, L2_gnn_W_out_b, L2_gnn_ln_gamma, L2_gnn_ln_beta)
    h = jnp.maximum(_layernorm(x, axis=-1), 0.0)
    x = x + _L3_gnn_ref(h, edge_index, L3_gnn_W1_l, L3_gnn_b1, L3_gnn_W1_r, L3_gnn_W2_l, L3_gnn_b2, L3_gnn_W2_r)
    return x

_drawn_inputs = setup_inputs


def setup_inputs(seed=0):
    import zlib

    import numpy as np

    out = dict(_drawn_inputs(seed))
    spreads = {'L1_gnn_b1': (0.0, 0.1),
     'L1_gnn_b2': (0.0, 0.1),
     'L1_gnn_ln_gamma': (1.0, 0.2),
     'L1_gnn_ln_beta': (0.0, 0.1),
     'L2_gnn_W_proj_b': (0.0, 0.1),
     'L2_gnn_W_out_b': (0.0, 0.1),
     'L2_gnn_ln_gamma': (1.0, 0.2),
     'L2_gnn_ln_beta': (0.0, 0.1),
     'L3_gnn_b1': (0.0, 0.1),
     'L3_gnn_b2': (0.0, 0.1)}
    factors = {}
    for name, (base, spread) in spreads.items():
        noise = np.random.default_rng([zlib.crc32(name.encode()), seed]).standard_normal(out[name].shape)
        drawn = base * np.exp(spread * noise) if base else spread * noise
        out[name] = jnp.asarray(drawn.astype(out[name].dtype))
    for name, factor in factors.items():
        out[name] = (out[name] * factor).astype(out[name].dtype)
    return out
```

```python
from contextlib import ExitStack

import numpy as np

import concourse.bass as bass
from concourse import mybir

P = 128
T = 4
R = 4
EPS = 1e-5
TABLES = 2
HEADS = 4
FAR = 1e30

F32 = mybir.dt.float32
I32 = mybir.dt.int32
U32 = mybir.dt.uint32
ALU = mybir.AluOpType
ACT = mybir.ActivationFunctionType
AX = mybir.AxisListType


class Step:

    def __init__(self, i, b):
        self.i, self.b = i, b
        self.static = isinstance(i, int)
        self.n = i * R + b

    def has(self, back):
        return not self.static or self.b >= back

    def ring(self, depth=R):
        return self.b % depth

    def count(self, per_step=1, back=0):
        return self.i * (R * per_step) + (self.b + 1 - back) * per_step

    def landed(self, per_step=1, back=0):
        return self.i * per_step + ((self.b - back) // R + 1) * per_step

    def tiles(self, width=1):
        return bass.ds(self.i * (R * T * width) + self.b * T * width, T * width)


def slots(eng, steps, most):
    first = most + R
    rounds = max((steps - first) // R, 0)
    for u in range(min(first, steps + most)):
        yield Slot(0, u, steps)
    if rounds:
        with eng.Fori(0, rounds) as i:
            for k in range(R):
                yield Slot(i, first + k, steps)
    for u in range(first + rounds * R, steps + most):
        yield Slot(0, u, steps)


class Slot:
    def __init__(self, i, u, steps):
        self.i, self.u, self.steps = i, u, steps

    def step(self, lag):
        if isinstance(self.i, int) and not 0 <= self.u - lag < self.steps:
            return None
        return Step(self.i, self.u - lag)


class Scope:

    def __init__(self, nc, ctx, name):
        self.nc, self.ctx, self.name, self.all_sems = nc, ctx, name, []

    def sb(self, name, shape, dt=F32):
        return self.ctx.enter_context(self.nc.sbuf_tensor(f"{self.name}_{name}", shape, dt))

    def ps(self, name, shape):
        return self.ctx.enter_context(self.nc.psum_tensor(f"{self.name}_{name}", shape, F32))

    def sem(self, name):
        self.all_sems.append(self.ctx.enter_context(self.nc.semaphore(f"{self.name}_{name}")))
        return self.all_sems[-1]

    def sems(self, name, n=R):
        return [self.sem(f"{name}{k}") for k in range(n)]


    def block(self):
        self.nc.gpsimd.dma_reset()
        for sem in self.all_sems:
            self.nc.gpsimd.sem_clear(sem)
        self.nc.all_engine_barrier()
        return self.ctx.enter_context(self.nc.Block())


def rows(table):
    return table.rearrange("(p c) d -> p c d", p=P)


def table_rows(table, C):
    return rows(table[0:P * C, :])


def all_landed(eng, sems, steps, per_step):
    for k, sem in enumerate(sems):
        if k < steps:
            eng.wait_ge(sem, len(range(k, steps, R)) * per_step)


def over(vector):
    return vector[:, :].unsqueeze(1).to_broadcast([P, T, P])


def apart(eng, st, passed):
    if not st.static:
        eng.sem_inc(passed, 1)


def zero_step(sp, g, C, tables, st, zeroed):
    for table in tables:
        W = table.shape[1]
        sp.dma_start(table_rows(table, C)[:, st.tiles(), :],
                     g["zeros"][:, 0:T * W].rearrange("p (t w) -> p t w", t=T)).then_inc(zeroed, 16)


def zero_spare(sp, g, C, tables, zeroed):
    for table in tables:
        sp.dma_start(table[P * C:P * C + P, :], g["zeros"][:, 0:table.shape[1]]).then_inc(zeroed, 16)


def zeroings(tables, steps):
    return 16 * len(tables) * (steps + 1)


def setup(nc, g, C):
    with ExitStack() as ctx:
        s = Scope(nc, ctx, "setup")
        last_first = s.sb("last_first", [P, 2])
        falls, fall = s.sb("falls", [P, C]), s.sb("fall", [P, 2])
        edge_ids, cross, total = s.sb("edge_ids", [1, 2, P]), s.sb("cross", [1, P]), s.sb("total", [1, 4])
        ids_row, fall_sum = s.ps("ids_row", [1, 2, P]), s.ps("fall_sum", [1, 1])
        loaded, made, chain = s.sem("loaded"), s.sem("made"), s.sem("chain")
        spare_ready, constants, turned = s.sem("spare_ready"), s.sem("constants"), s.sem("turned")
        copied, kept = s.sem("copied"), s.sem("kept")
        loads = [(g["src_i"][:, :], g["src"].rearrange("(p c) -> p c", p=P)),
                 (g["dst_i"][:, :], g["dst"].rearrange("(p c) -> p c", p=P)),
                 (g["weight"][:, :], g["edge_weight"].rearrange("(p c) -> p c", p=P))] + g["loads"]
        block = s.block()

        @block.sync
        def _(sp):
            for out, in_ in loads:
                sp.dma_start(out, in_).then_inc(loaded, 16)
            sp.wait_ge(loaded, 16 * len(loads))
            sp.wait_ge(copied, 8)
            sp.dma_start(g["unsorted"], g["unsorted_i"][0:1, 0:1]).then_inc(kept, 16)
            sp.wait_ge(kept, 16)

        @block.gpsimd
        def _(pool):
            pool.memset(g["ident"][:, :], 0.0).then_inc(made, 1)
            pool.memset(g["before"][:, :], 1.0).then_inc(made, 1)
            pool.memset(g["ones"][:, :], 1.0)
            pool.memset(g["zeros"][:, :], 0.0)
            pool.memset(g["minus_half"][:, :], -0.5)
            pool.iota(g["spare_i"][:, :], [[0, 1]], base=P * C, channel_multiplier=1).then_inc(spare_ready, 1)
            pool.wait_ge(made, 2)
            pool.affine_select(out=g["ident"][:, :], in_=g["ident"][:, :], compare_op=ALU.not_equal,
                               fill=1.0, base=0, pattern=[[-1, P]], channel_multiplier=1)
            pool.affine_select(out=g["before"][:, :], in_=g["before"][:, :], compare_op=ALU.is_gt,
                               fill=0.0, base=0, pattern=[[-1, P]], channel_multiplier=1).then_inc(constants, 1)

        @block.vector
        def _(dve):
            dve.wait_ge(loaded, 16 * len(loads))
            dve.wait_ge(spare_ready, 1)
            dve.tensor_copy(g["src_f"][:, :], g["src_i"][:, :])
            dve.tensor_copy(g["dst_f"][:, :], g["dst_i"][:, :])
            dve.tensor_copy(g["spare_f"][:, :], g["spare_i"][:, :]).then_inc(chain, 1)
            dve.wait_ge(chain, 1)
            for key in ("src", "dst"):
                dve.tensor_scalar(g[key + "_spare"][:, :], g[key + "_f"][:, :], -1.0, g["spare_f"][:, 0:1],
                                  ALU.mult, ALU.add)
            dve.tensor_copy(last_first[:, 0:1], g["dst_f"][:, C - 1:C])
            dve.tensor_copy(last_first[:, 1:2], g["dst_f"][:, 0:1]).then_inc(copied, 1)
            dve.tensor_tensor(falls[:, 0:C - 1], g["dst_f"][:, 0:C - 1], g["dst_f"][:, 1:C],
                              ALU.is_gt).then_inc(copied, 1)
            dve.wait_ge(copied, 2)
            dve.tensor_reduce(fall[:, 0:1], falls[:, 0:C - 1], AX.X, ALU.add).then_inc(copied, 1)
            dve.wait_ge(turned, 1)
            dve.tensor_copy(edge_ids[:, :, :], ids_row[:, :, :]).then_inc(copied, 1)
            dve.wait_ge(copied, 4)
            dve.tensor_tensor(cross[:, 0:P - 1], edge_ids[:, 0, 0:P - 1], edge_ids[:, 1, 1:P], ALU.is_gt).then_inc(copied, 1)
            dve.wait_ge(copied, 5)
            dve.tensor_reduce(total[:, 0:1], cross[:, 0:P - 1], AX.X, ALU.add).then_inc(copied, 1)
            dve.wait_ge(copied, 6)
            dve.wait_ge(turned, 2)
            dve.tensor_tensor(total[:, 1:2], total[:, 0:1], fall_sum[:, :], ALU.add).then_inc(copied, 1)
            dve.wait_ge(copied, 7)
            dve.tensor_scalar(g["unsorted_i"][0:1, 0:1], total[:, 1:2], 1.0, None, ALU.min).then_inc(copied, 1)

        @block.tensor
        def _(pe):
            pe.wait_ge(constants, 1)
            pe.wait_ge(copied, 1)
            for k in range(2):
                last = pe.transpose(ids_row[:, k, :], last_first[:, k:k + 1], g["ident"][:, :])
            last.then_inc(turned, 1)
            pe.wait_ge(copied, 3)
            pe.matmul(fall_sum[:, :], fall[:, 0:1], g["ones"][:, 0:1], start=True, stop=True).then_inc(turned, 1)


class Norm:

    def __init__(self, s, name, minus_half, passed):
        self.minus_half, self.passed = minus_half, passed
        self.stats = s.sb(name + "_stats", [P, 2, T, 6])
        self.moments = s.sb(name + "_moments", [P, R, T, 2])
        self.var, self.rstd, self.offset = (s.sb(f"{name}_{n}", [P, R, T]) for n in ("var", "rstd", "offset"))
        self.stats_ready, self.moments_ready = s.sem(name + "_stats_ready"), s.sem(name + "_moments_ready")
        self.var_ready, self.rstd_ready = s.sem(name + "_var_ready"), s.sem(name + "_rstd_ready")
        self.offset_ready, self.normed = s.sem(name + "_offset_ready"), s.sem(name + "_normed")

    def statistics(self, dve, st, x):
        r, q = st.ring(), st.ring(2)
        for t in range(T):
            last = dve.bn_stats(self.stats[:, q, t, :], x[:, r, t, :])
        last.then_inc(self.stats_ready, 1)
        if st.has(R):
            dve.wait_ge(self.offset_ready, st.count(back=R))
        dve.wait_ge(self.stats_ready, st.count())
        apart(dve, st, self.passed)
        for t in range(T):
            last = dve.bn_aggr(self.moments[:, r, t, :], self.stats[:, q, t, :])
        last.then_inc(self.moments_ready, 1)

    def power(self, pool, st):
        r = st.ring()
        if st.has(R):
            pool.wait_ge(self.normed, st.count(back=R))
        pool.wait_ge(self.moments_ready, st.count())
        apart(pool, st, self.passed)
        pool.tensor_scalar(self.var[:, r, :], self.moments[:, r, :, 1], EPS, None, ALU.add).then_inc(self.var_ready, 1)
        pool.wait_ge(self.var_ready, st.count())
        pool.tensor_tensor(self.rstd[:, r, :], self.var[:, r, :], self.minus_half[:, 0:T],
                           ALU.pow).then_inc(self.rstd_ready, 1)

    def shift(self, dve, st):
        r = st.ring()
        if st.has(R):
            dve.wait_ge(self.normed, st.count(back=R))
        dve.wait_ge(self.rstd_ready, st.count())
        dve.scalar_tensor_tensor(out=self.offset[:, r, :], in0=self.moments[:, r, :, 0], scalar=-1.0,
                                 in1=self.rstd[:, r, :], op0=ALU.mult, op1=ALU.mult).then_inc(self.offset_ready, 1)

    def apply(self, act, st, out, x, func):
        r = st.ring()
        act.wait_ge(self.offset_ready, st.count())
        for t in range(T):
            last = act.activation(out[:, r, t, :], x[:, r, t, :], func, bias=self.offset[:, r, t:t + 1],
                                  scale=self.rstd[:, r, t:t + 1])
        last.then_inc(self.normed, 1)


def node_norm(nc, g, C, zero):
    steps = C // T
    with ExitStack() as ctx:
        s = Scope(nc, ctx, "norm")
        x, h = s.sb("x", [P, R, T, P]), s.sb("h", [P, R, T, P])
        x_landed, h_stored, zeroed = s.sems("x_landed"), s.sems("h_stored"), s.sem("zeroed")
        norm = Norm(s, "ln", g["minus_half"], g["passed"])
        block = s.block()

        @block.sync
        def _(sp):
            zero_spare(sp, g, C, zero, zeroed)
            for slot in slots(sp, steps, 3):
                if st := slot.step(3):
                    sp.wait_ge(norm.normed, st.count())
                    sp.dma_start(rows(g["h0"])[:, st.tiles(), :], h[:, st.ring()]).then_inc(h_stored[st.ring()], 16)
                if st := slot.step(0):
                    if st.has(R):
                        sp.wait_ge(norm.normed, st.count(back=R))
                    sp.dma_start(x[:, st.ring()], rows(g["x"])[:, st.tiles(), :]).then_inc(x_landed[st.ring()], 16)
                    zero_step(sp, g, C, zero, st, zeroed)
            all_landed(sp, h_stored, steps, 16)
            sp.wait_ge(zeroed, zeroings(zero, steps))

        @block.vector
        def _(dve):
            for slot in slots(dve, steps, 2):
                if st := slot.step(2):
                    norm.shift(dve, st)
                if st := slot.step(1):
                    dve.wait_ge(x_landed[st.ring()], st.landed(16))
                    norm.statistics(dve, st, x)

        @block.gpsimd
        def _(pool):
            for slot in slots(pool, steps, 1):
                if st := slot.step(1):
                    norm.power(pool, st)

        @block.scalar
        def _(act):
            for slot in slots(act, steps, 2):
                if st := slot.step(2):
                    if st.has(R):
                        act.wait_ge(h_stored[st.ring()], st.landed(16, back=R))
                    norm.apply(act, st, h, x, ACT.Relu)


def edge_sum(nc, g, C, name, tables, by, gather=None, load=None, weighted=False, first=False, extra=None, zero=()):
    steps = C // T
    D = P
    W = D + {None: 0, "ones": 1, "exp": HEADS}[extra]
    adds = 16 * T // TABLES
    moved = 16 * T if gather else 16
    scaled = weighted or extra == "exp"
    with ExitStack() as ctx:
        s = Scope(nc, ctx, name)
        gather_idx = s.sb("gather_idx", [P, R, T], I32)
        target = s.sb("target", [P, R, T], I32)
        ids = s.sb("ids", [P, R, T])
        factor = s.sb("factor", [P, R, T])
        more = s.sb("more", [P, R, T, HEADS])
        messages = s.sb("messages", [P, R, T, D])
        same = s.sb("same", [P, R, T, P])
        earlier = s.sb("earlier", [P, 2, T, P])
        n_earlier, shift = s.sb("n_earlier", [P, 2, T]), s.sb("shift", [P, 2, T])
        totals = s.sb("totals", [P, R, T, W])
        id_rows = s.ps("id_rows", [P, 2, T, P])
        sums = s.ps("sums", [P, 2, T, 256])

        staged, gathered, scaled_ready = s.sem("staged"), s.sems("gathered"), s.sem("scaled_ready")
        id_rows_ready, same_ready, earlier_ready = s.sem("id_rows_ready"), s.sem("same_ready"), s.sem("earlier_ready")
        counted, shift_ready, target_ready = s.sem("counted"), s.sem("shift_ready"), s.sem("target_ready")
        target_kept, summed, totals_ready = s.sem("target_kept"), s.sem("summed"), s.sem("totals_ready")
        added = [s.sem(f"added{k}") for k in range(TABLES)]
        zeroed = s.sem("zeroed")
        block = s.block()

        @block.sync
        def _(sp):
            zero_spare(sp, g, C, zero, zeroed)
            for slot in slots(sp, steps, 1):
                if load is not None and (st := slot.step(1)):
                    if st.has(R):
                        sp.wait_ge(summed, st.count(back=R))
                    sp.dma_start(messages[:, st.ring()], rows(load)[:, st.tiles(), :]).then_inc(gathered[st.ring()], 16)
                if zero and (st := slot.step(0)):
                    if st.has(R):
                        sp.wait_ge(summed, st.count(back=R))
                    zero_step(sp, g, C, zero, st, zeroed)
            if zero:
                sp.wait_ge(zeroed, zeroings(zero, steps))

        @block.scalar
        def _(act):
            for slot in slots(act, steps, 3):
                if st := slot.step(3):
                    act.wait_ge(summed, st.count())
                    if st.has(R):
                        for k in range(TABLES):
                            act.wait_ge(added[k], st.count(adds, back=R))
                    act.activation(totals[:, st.ring()], sums[:, st.ring(2), :, 0:W], ACT.Copy).then_inc(totals_ready, 1)
                if weighted and (st := slot.step(2)):
                    r = st.ring()
                    act.wait_ge(gathered[r], st.landed(moved))
                    for t in range(T):
                        last = act.activation(messages[:, r, t, :], messages[:, r, t, :], ACT.Copy,
                                              scale=factor[:, r, t:t + 1])
                    last.then_inc(scaled_ready, 1)
                if st := slot.step(0):
                    r = st.ring()
                    if st.has(R):
                        act.wait_ge(summed, st.count(back=R))
                        act.wait_ge(same_ready, st.count(back=R))
                        if first:
                            act.wait_ge(target_ready, st.count(back=R))
                            act.wait_ge(target_kept, st.count(back=R))
                        if scaled:
                            act.wait_ge(scaled_ready, st.count(back=R))
                        if gather:
                            act.wait_ge(gathered[r], st.landed(moved, back=R))
                        if not first:
                            for k in range(TABLES):
                                act.wait_ge(added[k], st.count(adds, back=R))
                    if gather:
                        act.activation(gather_idx[:, r, :], gather[1][:, st.tiles()], ACT.Copy)
                    if not first:
                        act.activation(target[:, r, :], g[by + "_target"][:, st.tiles()], ACT.Copy)
                    if weighted:
                        act.activation(factor[:, r, :], g["weight"][:, st.tiles()], ACT.Copy)
                    if extra == "exp":
                        act.activation(more[:, r].rearrange("p t h -> p (t h)"), g["exps"][:, st.tiles(HEADS)], ACT.Copy)
                    act.activation(ids[:, r, :], g[by + "_f"][:, st.tiles()], ACT.Copy).then_inc(staged, 1)

        @block.gpsimd
        def _(pool):
            for slot in slots(pool, steps, 4):
                for t in range(T):
                    if st := slot.step(4):
                        r, k = st.ring(), t % TABLES
                        if t == 0:
                            pool.wait_ge(totals_ready, st.count())
                            pool.wait_ge(target_ready if first else staged, st.count())
                        if t >= TABLES or st.has(1):
                            pool.wait_ge(added[k], st.count(adds, back=1) + 16 * (t // TABLES))
                        apart(pool, st, g["passed"])
                        pool.indirect_dma_start(
                            out=tables[k], out_offset=bass.IndirectOffsetOnAxis(target[:, r, t:t + 1], 0),
                            in_=totals[:, r, t, :], in_offset=None, compute_op=ALU.add,
                        ).then_inc(added[k], 16)
                    if gather and (st := slot.step(1)):
                        r = st.ring()
                        if t == 0:
                            if st.has(R):
                                pool.wait_ge(summed, st.count(back=R))
                            pool.wait_ge(staged, st.count())
                            apart(pool, st, g["passed"])
                        pool.indirect_dma_start(
                            out=messages[:, r, t, :], out_offset=None, in_=gather[0],
                            in_offset=bass.IndirectOffsetOnAxis(gather_idx[:, r, t:t + 1], 0),
                        ).then_inc(gathered[r], 16)
            for k in range(TABLES):
                pool.wait_ge(added[k], steps * adds)
            if gather:
                all_landed(pool, gathered, steps, moved)

        @block.tensor
        def _(pe):
            for slot in slots(pe, steps, 3):
                if st := slot.step(3):
                    r, q = st.ring(), st.ring(2)
                    pe.wait_ge(same_ready, st.count())
                    if scaled:
                        pe.wait_ge(scaled_ready, st.count())
                    else:
                        pe.wait_ge(gathered[r], st.landed(moved))
                    if st.has(2):
                        pe.wait_ge(totals_ready, st.count(back=2))
                    for t in range(T):
                        last = pe.matmul(sums[:, q, t, 0:D], same[:, r, t, :], messages[:, r, t, :], start=True, stop=True)
                        if extra:
                            cols = g["ones"][:, 0:1] if extra == "ones" else more[:, r, t, :]
                            last = pe.matmul(sums[:, q, t, D:W], same[:, r, t, :], cols, start=True, stop=True)
                    last.then_inc(summed, 1)
                if st := slot.step(1):
                    r, q = st.ring(), st.ring(2)
                    pe.wait_ge(staged, st.count())
                    if st.has(2):
                        pe.wait_ge(same_ready, st.count(back=2))
                    for t in range(T):
                        last = pe.matmul(id_rows[:, q, t, :], ids[:, r, t:t + 1].to_broadcast([P, P]),
                                         g["ident"][:, :], start=True, stop=True)
                    last.then_inc(id_rows_ready, 1)

        @block.vector
        def _(dve):
            for slot in slots(dve, steps, 2):
                if st := slot.step(2):
                    r, q = st.ring(), st.ring(2)
                    dve.wait_ge(id_rows_ready, st.count())
                    if st.has(R):
                        dve.wait_ge(summed, st.count(back=R))
                    dve.tensor_tensor(same[:, r], id_rows[:, q], ids[:, r].unsqueeze(2).to_broadcast([P, T, P]),
                                      ALU.is_equal).then_inc(same_ready, 1)
                    if first:
                        dve.wait_ge(same_ready, st.count())
                        dve.tensor_tensor(earlier[:, q], same[:, r],
                                          g["before"][:, :].unsqueeze(1).to_broadcast([P, T, P]),
                                          ALU.mult).then_inc(earlier_ready, 1)
                        dve.wait_ge(earlier_ready, st.count())
                        dve.tensor_reduce(n_earlier[:, q, :], earlier[:, q], AX.X, ALU.add).then_inc(counted, 1)
                        dve.wait_ge(counted, st.count())
                        dve.scalar_tensor_tensor(out=shift[:, q, :], in0=n_earlier[:, q, :], scalar=1.0,
                                                 in1=g[by + "_spare"][:, st.tiles()], op0=ALU.min, op1=ALU.mult
                                                 ).then_inc(shift_ready, 1)
                        dve.wait_ge(shift_ready, st.count())
                        if st.has(R):
                            for k in range(TABLES):
                                dve.wait_ge(added[k], st.count(adds, back=R))
                        dve.tensor_tensor(target[:, r, :], shift[:, q, :], ids[:, r, :], ALU.add).then_inc(target_ready, 1)
                        dve.tensor_tensor(g[by + "_target"][:, st.tiles()], shift[:, q, :], ids[:, r, :],
                                          ALU.add).then_inc(target_kept, 1)
                    if extra == "exp":
                        dve.wait_ge(gathered[r], st.landed(moved))
                        view = messages[:, r].rearrange("p t (h d) -> p (t h) d", h=HEADS)
                        factors = more[:, r].rearrange("p t h -> p (t h)").unsqueeze(2)
                        dve.tensor_tensor(view, view, factors.to_broadcast([P, T * HEADS, D // HEADS]),
                                          ALU.mult).then_inc(scaled_ready, 1)
            if first:
                dve.wait_ge(target_kept, steps)


def node_rel(nc, g, C, zero):
    steps = C // T
    with ExitStack() as ctx:
        s = Scope(nc, ctx, "rel")
        a, b, x, x1, h, xh = (s.sb(k, [P, R, T, P]) for k in ("a", "b", "x", "x1", "h", "xh"))
        aT = s.sb("aT", [P, 2, T, P])
        aT_ps, product_ps = s.ps("aT_ps", [P, 2, T, P]), s.ps("product_ps", [P, 2, T, P])
        a_landed, b_landed, x_landed = s.sems("a_landed"), s.sems("b_landed"), s.sems("x_landed")
        h_stored, xh_stored, zeroed = s.sems("h_stored"), s.sems("xh_stored"), s.sem("zeroed")
        agg_ready, turned, aT_ready, product = s.sem("agg_ready"), s.sem("turned"), s.sem("aT_ready"), s.sem("product")
        x1_ready, xh_ready = s.sem("x1_ready"), s.sem("xh_ready")
        norm = Norm(s, "ln", g["minus_half"], g["passed"])
        tables = [table_rows(t, C) for t in g["agg_rel"]]
        block = s.block()

        @block.sync
        def _(sp):
            zero_spare(sp, g, C, zero, zeroed)
            for slot in slots(sp, steps, 8):
                if st := slot.step(8):
                    sp.wait_ge(xh_ready, st.count())
                    sp.dma_start(rows(g["xh"])[:, st.tiles(), :], xh[:, st.ring()]).then_inc(xh_stored[st.ring()], 16)
                if st := slot.step(7):
                    sp.wait_ge(norm.normed, st.count())
                    sp.dma_start(rows(g["h1"])[:, st.tiles(), :], h[:, st.ring()]).then_inc(h_stored[st.ring()], 16)
                if st := slot.step(3):
                    if st.has(R):
                        sp.wait_ge(x1_ready, st.count(back=R))
                    sp.dma_start(x[:, st.ring()], rows(g["x"])[:, st.tiles(), :]).then_inc(x_landed[st.ring()], 16)
                if st := slot.step(0):
                    r = st.ring()
                    if st.has(R):
                        sp.wait_ge(turned, st.count(back=R))
                        sp.wait_ge(agg_ready, st.count(back=R))
                    sp.dma_start(a[:, r], tables[0][:, st.tiles(), :]).then_inc(a_landed[r], 16)
                    sp.dma_start(b[:, r], tables[1][:, st.tiles(), :]).then_inc(b_landed[r], 16)
                    zero_step(sp, g, C, zero, st, zeroed)
            all_landed(sp, h_stored, steps, 16)
            all_landed(sp, xh_stored, steps, 16)
            if zero:
                sp.wait_ge(zeroed, zeroings(zero, steps))

        @block.vector
        def _(dve):
            for slot in slots(dve, steps, 6):
                if st := slot.step(6):
                    norm.shift(dve, st)
                if st := slot.step(4):
                    r = st.ring()
                    dve.wait_ge(product, st.count())
                    dve.wait_ge(x_landed[r], st.landed(16))
                    if st.has(R):
                        dve.wait_ge(norm.normed, st.count(back=R))
                        dve.wait_ge(xh_ready, st.count(back=R))
                    dve.scalar_tensor_tensor(out=x1[:, r], in0=product_ps[:, st.ring(2)], scalar=0.0, in1=x[:, r],
                                             op0=ALU.max, op1=ALU.add).then_inc(x1_ready, 1)
                    dve.wait_ge(x1_ready, st.count())
                    norm.statistics(dve, st, x1)
                if st := slot.step(1):
                    r = st.ring()
                    dve.wait_ge(a_landed[r], st.landed(16))
                    dve.wait_ge(b_landed[r], st.landed(16))
                    dve.tensor_tensor(a[:, r], a[:, r], b[:, r], ALU.add).then_inc(agg_ready, 1)

        @block.gpsimd
        def _(pool):
            for slot in slots(pool, steps, 7):
                if st := slot.step(7):
                    r = st.ring()
                    pool.wait_ge(norm.normed, st.count())
                    if st.has(R):
                        pool.wait_ge(xh_stored[r], st.landed(16, back=R))
                    pool.tensor_tensor(xh[:, r], x1[:, r], h[:, r], ALU.add).then_inc(xh_ready, 1)
                if st := slot.step(4):
                    norm.power(pool, st)

        @block.scalar
        def _(act):
            for slot in slots(act, steps, 6):
                if st := slot.step(6):
                    if st.has(R):
                        act.wait_ge(h_stored[st.ring()], st.landed(16, back=R))
                        act.wait_ge(xh_ready, st.count(back=R))
                    norm.apply(act, st, h, x1, ACT.Relu)
                if st := slot.step(2):
                    act.wait_ge(turned, st.count())
                    if st.has(2):
                        act.wait_ge(product, st.count(back=2))
                    act.activation(aT[:, st.ring(2)], aT_ps[:, st.ring(2)], ACT.Copy).then_inc(aT_ready, 1)

        @block.tensor
        def _(pe):
            for slot in slots(pe, steps, 3):
                if st := slot.step(3):
                    q = st.ring(2)
                    pe.wait_ge(aT_ready, st.count())
                    if st.has(2):
                        pe.wait_ge(x1_ready, st.count(back=2))
                    for t in range(T):
                        last = pe.matmul(product_ps[:, q, t, :], aT[:, q, t, :], g["w_rel"][:, :], start=True, stop=True)
                    last.then_inc(product, 1)
                if st := slot.step(2):
                    pe.wait_ge(agg_ready, st.count())
                    if st.has(2):
                        pe.wait_ge(aT_ready, st.count(back=2))
                    for t in range(T):
                        last = pe.transpose(aT_ps[:, st.ring(2), t, :], a[:, st.ring(), t, :], g["ident"][:, :])
                    last.then_inc(turned, 1)


def node_mlp(nc, g, C):
    steps = C // T
    with ExitStack() as ctx:
        s = Scope(nc, ctx, "mlp")
        a, b, x, h, z, zn, base, x2, h2, y = (s.sb(k, [P, R, T, P]) for k in (
            "a", "b", "x", "h", "z", "zn", "base", "x2", "h2", "y"))
        inT = s.sb("inT", [P, 2, 2, T * P])
        hid, h2T = s.sb("hid", [P, 2, 2, T * P]), s.sb("h2T", [P, 2, T, P])
        hT_ps, aT_ps, h2T_ps = (s.ps(k, [P, T, P]) for k in ("hT_ps", "aT_ps", "h2T_ps"))
        hid_ps, out_ps, y_ps = s.ps("hid_ps", [P, 2, T * P]), s.ps("out_ps", [P, 2, T, P]), s.ps("y_ps", [P, T, P])
        a_landed, b_landed, x_landed, h_landed = (s.sems(k + "_landed") for k in "abxh")
        x2_stored, h2_stored, y_stored = (s.sems(k + "_stored") for k in ("x2", "h2", "y"))
        agg_ready, h_turned, a_turned, hT_ready, aT_ready, hid_product, hid_ready = (s.sem(k) for k in (
            "agg_ready", "h_turned", "a_turned", "hT_ready", "aT_ready", "hid_product", "hid_ready"))
        out_product, z_ready, base_ready, gammaed, x2_ready = (s.sem(k) for k in (
            "out_product", "z_ready", "base_ready", "gammaed", "x2_ready"))
        h2_turned, h2T_ready, y_product, y_ready = (s.sem(k) for k in ("h2_turned", "h2T_ready", "y_product", "y_ready"))
        norm1, norm2 = (Norm(s, k, g["minus_half"], g["passed"]) for k in ("ln1", "ln2"))
        tables = [table_rows(t, C) for t in g["agg_mlp"]]
        block = s.block()

        @block.sync
        def _(sp):
            for slot in slots(sp, steps, 12):
                if st := slot.step(12):
                    sp.wait_ge(y_ready, st.count())
                    sp.dma_start(rows(g["y2"])[:, st.tiles(), :], y[:, st.ring()]).then_inc(y_stored[st.ring()], 16)
                if st := slot.step(9):
                    sp.wait_ge(norm2.normed, st.count())
                    sp.dma_start(rows(g["h2"])[:, st.tiles(), :], h2[:, st.ring()]).then_inc(h2_stored[st.ring()], 16)
                if st := slot.step(8):
                    sp.wait_ge(x2_ready, st.count())
                    sp.dma_start(rows(g["x2"])[:, st.tiles(), :], x2[:, st.ring()]).then_inc(x2_stored[st.ring()], 16)
                if st := slot.step(4):
                    if st.has(R):
                        sp.wait_ge(base_ready, st.count(back=R))
                    sp.dma_start(x[:, st.ring()], rows(g["xh"])[:, st.tiles(), :]).then_inc(x_landed[st.ring()], 16)
                if st := slot.step(0):
                    r = st.ring()
                    if st.has(R):
                        sp.wait_ge(h_turned, st.count(back=R))
                        sp.wait_ge(a_turned, st.count(back=R))
                        sp.wait_ge(agg_ready, st.count(back=R))
                    sp.dma_start(h[:, r], rows(g["h1"])[:, st.tiles(), :]).then_inc(h_landed[r], 16)
                    sp.dma_start(a[:, r], tables[0][:, st.tiles(), :]).then_inc(a_landed[r], 16)
                    sp.dma_start(b[:, r], tables[1][:, st.tiles(), :]).then_inc(b_landed[r], 16)
            for stored in (x2_stored, h2_stored, y_stored):
                all_landed(sp, stored, steps, 16)

        @block.vector
        def _(dve):
            for slot in slots(dve, steps, 11):
                if st := slot.step(11):
                    dve.wait_ge(y_product, st.count())
                    if st.has(R):
                        dve.wait_ge(y_stored[st.ring()], st.landed(16, back=R))
                    dve.tensor_tensor(y[:, st.ring()], y_ps[:, :, :], over(g["b_proj"]), ALU.add).then_inc(y_ready, 1)
                if st := slot.step(8):
                    norm2.shift(dve, st)
                if st := slot.step(7):
                    r = st.ring()
                    dve.wait_ge(norm1.normed, st.count())
                    dve.tensor_tensor(zn[:, r], zn[:, r], over(g["gamma_mlp"]), ALU.mult).then_inc(gammaed, 1)
                    dve.wait_ge(gammaed, st.count())
                    dve.wait_ge(base_ready, st.count())
                    if st.has(R):
                        dve.wait_ge(x2_stored[r], st.landed(16, back=R))
                        dve.wait_ge(norm2.normed, st.count(back=R))
                    dve.tensor_tensor(x2[:, r], zn[:, r], base[:, r], ALU.add).then_inc(x2_ready, 1)
                    dve.wait_ge(x2_ready, st.count())
                    norm2.statistics(dve, st, x2)
                if st := slot.step(6):
                    norm1.shift(dve, st)
                if st := slot.step(5):
                    r = st.ring()
                    dve.wait_ge(out_product, st.count())
                    if st.has(R):
                        dve.wait_ge(norm1.normed, st.count(back=R))
                    dve.tensor_tensor(z[:, r], out_ps[:, st.ring(2)], over(g["b2_mlp"]), ALU.add).then_inc(z_ready, 1)
                    dve.wait_ge(z_ready, st.count())
                    norm1.statistics(dve, st, z)
                if st := slot.step(1):
                    r = st.ring()
                    dve.wait_ge(a_landed[r], st.landed(16))
                    dve.wait_ge(b_landed[r], st.landed(16))
                    dve.tensor_tensor(a[:, r], a[:, r], b[:, r], ALU.add).then_inc(agg_ready, 1)

        @block.gpsimd
        def _(pool):
            for slot in slots(pool, steps, 7):
                if st := slot.step(7):
                    norm2.power(pool, st)
                if st := slot.step(6):
                    r = st.ring()
                    if st.has(R):
                        pool.wait_ge(x2_ready, st.count(back=R))
                    pool.wait_ge(x_landed[r], st.landed(16))
                    pool.tensor_tensor(base[:, r], x[:, r], over(g["beta_mlp"]), ALU.add).then_inc(base_ready, 1)
                if st := slot.step(5):
                    norm1.power(pool, st)

        @block.scalar
        def _(act):
            for slot in slots(act, steps, 9):
                if st := slot.step(9):
                    act.wait_ge(h2_turned, st.count())
                    if st.has(2):
                        act.wait_ge(y_product, st.count(back=2))
                    act.activation(h2T[:, st.ring(2)], h2T_ps[:, :, :], ACT.Copy).then_inc(h2T_ready, 1)
                if st := slot.step(8):
                    if st.has(R):
                        act.wait_ge(h2_stored[st.ring()], st.landed(16, back=R))
                        act.wait_ge(h2_turned, st.count(back=R))
                    norm2.apply(act, st, h2, x2, ACT.Relu)
                if st := slot.step(6):
                    if st.has(R):
                        act.wait_ge(x2_ready, st.count(back=R))
                    norm1.apply(act, st, zn, z, ACT.Identity)
                if st := slot.step(3):
                    act.wait_ge(hid_product, st.count())
                    if st.has(2):
                        act.wait_ge(out_product, st.count(back=2))
                    for m in range(2):
                        last = act.activation(hid[:, st.ring(2), m, :], hid_ps[:, m, :], ACT.Silu,
                                              bias=g["b1_mlp"][:, m:m + 1])
                    last.then_inc(hid_ready, 1)
                if st := slot.step(2):
                    q = st.ring(2)
                    if st.has(2):
                        act.wait_ge(hid_product, st.count(back=2))
                    act.wait_ge(h_turned, st.count())
                    act.activation(inT[:, q, 0, :], hT_ps[:, :, :].rearrange("p t n -> p (t n)"), ACT.Copy).then_inc(hT_ready, 1)
                    act.wait_ge(a_turned, st.count())
                    act.activation(inT[:, q, 1, :], aT_ps[:, :, :].rearrange("p t n -> p (t n)"), ACT.Copy).then_inc(aT_ready, 1)

        @block.tensor
        def _(pe):
            for slot in slots(pe, steps, 10):
                if st := slot.step(10):
                    pe.wait_ge(h2T_ready, st.count())
                    if st.has(1):
                        pe.wait_ge(y_ready, st.count(back=1))
                    for t in range(T):
                        last = pe.matmul(y_ps[:, t, :], h2T[:, st.ring(2), t, :], g["w_node"][:, :], start=True, stop=True)
                    last.then_inc(y_product, 1)
                if st := slot.step(9):
                    pe.wait_ge(norm2.normed, st.count())
                    if st.has(1):
                        pe.wait_ge(h2T_ready, st.count(back=1))
                    for t in range(T):
                        last = pe.transpose(h2T_ps[:, t, :], h2[:, st.ring(), t, :], g["ident"][:, :])
                    last.then_inc(h2_turned, 1)
                if st := slot.step(4):
                    q = st.ring(2)
                    pe.wait_ge(hid_ready, st.count())
                    if st.has(2):
                        pe.wait_ge(z_ready, st.count(back=2))
                    for t in range(T):
                        for m in range(2):
                            last = pe.matmul(out_ps[:, q, t, :], hid[:, q, m, t * P:(t + 1) * P], g["w2_mlp"][:, m, :],
                                             start=(m == 0), stop=(m == 1))
                    last.then_inc(out_product, 1)
                if st := slot.step(3):
                    q = st.ring(2)
                    pe.wait_ge(hT_ready, st.count())
                    pe.wait_ge(aT_ready, st.count())
                    if st.has(1):
                        pe.wait_ge(hid_ready, st.count(back=1))
                    for m in range(2):
                        for k in range(2):
                            last = pe.matmul(hid_ps[:, m, :], g["w1_mlp"][:, k, m * P:(m + 1) * P], inT[:, q, k, :],
                                             start=(k == 0), stop=(k == 1))
                    last.then_inc(hid_product, 1)
                if st := slot.step(2):
                    r = st.ring()
                    pe.wait_ge(h_landed[r], st.landed(16))
                    if st.has(1):
                        pe.wait_ge(hT_ready, st.count(back=1))
                    for t in range(T):
                        last = pe.transpose(hT_ps[:, t, :], h[:, r, t, :], g["ident"][:, :])
                    last.then_inc(h_turned, 1)
                    pe.wait_ge(agg_ready, st.count())
                    if st.has(1):
                        pe.wait_ge(aT_ready, st.count(back=1))
                    for t in range(T):
                        last = pe.transpose(aT_ps[:, t, :], a[:, r, t, :], g["ident"][:, :])
                    last.then_inc(a_turned, 1)


def edge_project(nc, g, C):
    steps, D, EF = C // T, P, g["edge_attr_64"].shape[1]
    moved = 16 * T
    with ExitStack() as ctx:
        s = Scope(nc, ctx, "proj")
        idx = s.sb("idx", [P, R, T], I32)
        y, xp, weighed = s.sb("y", [P, R, T, D]), s.sb("xp", [P, R, T, D]), s.sb("weighed", [P, 2, T, D])
        attr, attrT = s.sb("attr", [P, R, T, EF]), s.sb("attrT", [EF, 2, T, P])
        attrT_ps, product_ps = s.ps("attrT_ps", [EF, 2, T, P]), s.ps("product_ps", [P, 2, T, D])
        staged, gathered, landed = s.sem("staged"), s.sems("gathered"), s.sems("landed")
        turned, attrT_ready, product = s.sem("turned"), s.sem("attrT_ready"), s.sem("product")
        xp_ready, weighed_ready, scored, stored = s.sem("xp_ready"), s.sem("weighed_ready"), s.sem("scored"), s.sems("stored")
        block = s.block()

        @block.sync
        def _(sp):
            for slot in slots(sp, steps, 4):
                if st := slot.step(4):
                    sp.wait_ge(xp_ready, st.count())
                    sp.dma_start(rows(g["xp"])[:, st.tiles(), :], xp[:, st.ring()]).then_inc(stored[st.ring()], 16)
                if st := slot.step(0):
                    if st.has(R):
                        sp.wait_ge(turned, st.count(back=R))
                    sp.dma_start(attr[:, st.ring()], rows(g["edge_attr_64"])[:, st.tiles(), :]).then_inc(landed[st.ring()], 16)
            all_landed(sp, stored, steps, 16)

        @block.gpsimd
        def _(pool):
            for slot in slots(pool, steps, 1):
                if st := slot.step(1):
                    r = st.ring()
                    if st.has(R):
                        pool.wait_ge(xp_ready, st.count(back=R))
                    pool.wait_ge(staged, st.count())
                    apart(pool, st, g["passed"])
                    for t in range(T):
                        pool.indirect_dma_start(
                            out=y[:, r, t, :], out_offset=None, in_=g["y2"],
                            in_offset=bass.IndirectOffsetOnAxis(idx[:, r, t:t + 1], 0)).then_inc(gathered[r], 16)
            all_landed(pool, gathered, steps, moved)

        @block.scalar
        def _(act):
            for slot in slots(act, steps, 1):
                if st := slot.step(1):
                    act.wait_ge(turned, st.count())
                    if st.has(2):
                        act.wait_ge(product, st.count(back=2))
                    act.activation(attrT[:, st.ring(2)], attrT_ps[:, st.ring(2)], ACT.Copy).then_inc(attrT_ready, 1)
                if st := slot.step(0):
                    if st.has(R):
                        act.wait_ge(gathered[st.ring()], st.landed(moved, back=R))
                    act.activation(idx[:, st.ring(), :], g["src_i"][:, st.tiles()], ACT.Copy).then_inc(staged, 1)

        @block.tensor
        def _(pe):
            for slot in slots(pe, steps, 2):
                if st := slot.step(2):
                    q = st.ring(2)
                    pe.wait_ge(attrT_ready, st.count())
                    if st.has(2):
                        pe.wait_ge(xp_ready, st.count(back=2))
                    for t in range(T):
                        last = pe.matmul(product_ps[:, q, t, :], attrT[:, q, t, :], g["w_edge"][:, :], start=True, stop=True)
                    last.then_inc(product, 1)
                if st := slot.step(1):
                    if st.has(2):
                        pe.wait_ge(attrT_ready, st.count(back=2))
                    pe.wait_ge(landed[st.ring()], st.landed(16))
                    apart(pe, st, g["passed"])
                    for t in range(T):
                        last = pe.transpose(attrT_ps[:, st.ring(2), t, :], attr[:, st.ring(), t, :], g["ident"][:, :])
                    last.then_inc(turned, 1)

        @block.vector
        def _(dve):
            for slot in slots(dve, steps, 3):
                if st := slot.step(3):
                    r, q = st.ring(), st.ring(2)
                    dve.wait_ge(product, st.count())
                    dve.wait_ge(gathered[r], st.landed(moved))
                    if st.has(R):
                        dve.wait_ge(stored[r], st.landed(16, back=R))
                    dve.tensor_tensor(xp[:, r], product_ps[:, q], y[:, r], ALU.add).then_inc(xp_ready, 1)
                    dve.wait_ge(xp_ready, st.count())
                    dve.tensor_tensor(weighed[:, q], xp[:, r], over(g["attn"]), ALU.mult).then_inc(weighed_ready, 1)
                    dve.wait_ge(weighed_ready, st.count())
                    dve.tensor_reduce(g["scores"][:, st.tiles(HEADS)],
                                      weighed[:, q].rearrange("p t (h d) -> p (t h) d", h=HEADS), AX.X, ALU.add
                                      ).then_inc(scored, 1)
            dve.wait_ge(scored, steps)


def edge_exp_sorted(nc, g, C):
    H = HEADS
    with ExitStack() as ctx:
        s = Scope(nc, ctx, "sorted")
        link = s.sb("link", [P, C + 1])
        running, best = s.sb("running", [P, H, C]), s.sb("best", [P, H, C])
        ends = s.sb("ends", [P, 2])
        tails = s.sb("tails", [P, 2, H])
        carry = s.sb("carry", [P, H])
        ids, seam = s.sb("ids", [1, 2, P]), s.sb("seam", [1, P + 1])
        over_row = s.sb("over_row", [H, 2, P])
        row_scan, row_carry = s.sb("row_scan", [H, P]), s.sb("row_carry", [H, P])
        small = s.ps("small", [P, 512])
        dve_done, pe_done, act_done = s.sem("dve_done"), s.sem("pe_done"), s.sem("act_done")
        scores = g["scores"][:, :].rearrange("p (c h) -> p h c", h=H)
        exps = g["exps"][:, :].rearrange("p (c h) -> p h c", h=H)
        turns = []
        block = s.block()

        @block.vector
        def _(dve):
            n = [0]

            def then(instruction):
                n[0] += 1
                instruction.then_inc(dve_done, 1)
                dve.wait_ge(dve_done, n[0])

            def turned():
                turns.append(n[0])
                dve.wait_ge(pe_done, len(turns))

            dve.tensor_copy(ends[:, 0:1], g["dst_f"][:, 0:1])
            dve.memset(seam[:, :], -FAR)
            then(dve.tensor_copy(ends[:, 1:2], g["dst_f"][:, C - 1:C]))
            turned()
            then(dve.tensor_copy(ids[:, :, :], small[0:1, 0:2 * P].rearrange("o (k p) -> o k p", k=2)))
            then(dve.tensor_tensor(seam[:, 1:P], ids[:, 0, 1:P], ids[:, 1, 0:P - 1], ALU.not_equal))
            then(dve.tensor_scalar(seam[:, 1:P], seam[:, 1:P], -FAR, None, ALU.mult))
            turned()
            dve.tensor_copy(link[:, 0:1], small[:, 0:1])
            dve.tensor_copy(link[:, C:C + 1], small[:, 1:2])
            then(dve.tensor_tensor(link[:, 1:C], g["dst_f"][:, 1:C], g["dst_f"][:, 0:C - 1], ALU.not_equal))
            then(dve.tensor_scalar(link[:, 1:C], link[:, 1:C], -FAR, None, ALU.mult))
            for back in (False, True):
                order = slice(None, None, -1) if back else slice(None)
                links = link[:, 1:C + 1] if back else link[:, 0:C]
                source, result = (running, best) if back else (scores, running)
                for h in range(H):
                    last = dve.tensor_tensor_scan(result[:, h, :][:, order], links[:, order], source[:, h, :][:, order],
                                                  -FAR, ALU.add, ALU.max)
                then(last)
                then(dve.tensor_reduce(tails[:, 1, 0:1], links, AX.X, ALU.min))
                dve.tensor_copy(tails[:, 1, 1:H], tails[:, 1, 0:1].to_broadcast([P, H - 1]))
                end = 0 if back else C - 1
                then(dve.tensor_copy(tails[:, 0, :], result[:, :, end]))
                turned()
                then(dve.tensor_copy(over_row[:, :, :], small[0:H, 0:2 * P].rearrange("h (k p) -> h k p", k=2)))
                then(dve.tensor_tensor_scan(row_scan[:, order], over_row[:, 1, order], over_row[:, 0, order],
                                            -FAR, ALU.add, ALU.max))
                then(dve.memset(row_carry[:, :], -FAR))
                if back:
                    then(dve.tensor_copy(row_carry[:, 0:P - 1], row_scan[:, 1:P]))
                else:
                    then(dve.tensor_copy(row_carry[:, 1:P], row_scan[:, 0:P - 1]))
                turned()
                then(dve.tensor_copy(carry[:, :], small[:, 0:H]))
                for h in range(H):
                    last = dve.tensor_tensor_scan(result[:, h, :][:, order], links[:, order], source[:, h, :][:, order],
                                                  carry[:, h:h + 1], ALU.add, ALU.max)
                then(last)
            then(dve.tensor_tensor(exps, scores, best[:, :, :], ALU.subtract))
            turns.append(n[0])

        @block.tensor
        def _(pe):
            pe.wait_ge(dve_done, turns[0])
            for k in range(2):
                last = pe.transpose(small[0:1, k * P:(k + 1) * P], ends[:, k:k + 1], g["ident"][:, :])
            last.then_inc(pe_done, 1)
            pe.wait_ge(dve_done, turns[1])
            for k in range(2):
                last = pe.matmul(small[:, k:k + 1], seam[0:1, k:k + P], g["ones"][0:1, 0:1], start=True, stop=True)
            last.then_inc(pe_done, 1)
            for back in range(2):
                pe.wait_ge(dve_done, turns[2 + 2 * back])
                for k in range(2):
                    last = pe.transpose(small[0:H, k * P:(k + 1) * P], tails[:, k, :], g["ident"][:, :])
                last.then_inc(pe_done, 1)
                pe.wait_ge(dve_done, turns[3 + 2 * back])
                pe.transpose(small[:, 0:H], row_carry[:, :], g["ident"][0:H, 0:H]).then_inc(pe_done, 1)

        @block.scalar
        def _(act):
            act.wait_ge(dve_done, turns[6])
            act.activation(g["exps"][:, :], g["exps"][:, :], ACT.Exp).then_inc(act_done, 1)
            act.wait_ge(act_done, 1)


def edge_max(nc, g, C):
    steps, H = C // T, HEADS
    with ExitStack() as ctx:
        s = Scope(nc, ctx, "max")
        ids, target, own = s.sb("ids", [P, 2, T]), s.sb("target", [P, 2, T], I32), s.sb("own", [P, 2, T], I32)
        scores = s.sb("scores", [P, 2, T, H])
        away = s.sb("away", [P, 2, T, P])
        masked, best = s.sb("masked", [P, 2, T * H, P]), s.sb("best", [P, 2, T, H])
        seen, new = s.sb("seen", [P, 2, T, H]), s.sb("new", [P, 2, T, H])
        low, merged, lot = s.sb("low", [P, C * H]), s.sb("merged", [P, C * H]), s.sb("lot", [P, 2, C * H])
        id_rows, score_rows = s.ps("id_rows", [P, T, P]), s.ps("score_rows", [P, T * H, P])
        cleared, low_ready, staged, spread = s.sem("cleared"), s.sem("low_ready"), s.sem("staged"), s.sem("spread")
        same_ready, away_ready, masked_ready, best_ready = (s.sem(k) for k in (
            "same_ready", "away_ready", "masked_ready", "best_ready"))
        read, renewed, written = s.sem("read"), s.sem("renewed"), s.sem("written")
        lots, merging, final = s.sem("lots"), s.sem("merging"), s.sem("final")
        flat = [table_rows(m, C).rearrange("p c h -> p (c h)") for m in g["max_tables"]]
        block = s.block()

        @block.sync
        def _(sp):
            sp.wait_ge(low_ready, 1)
            for k, m in enumerate(g["max_tables"]):
                sp.dma_start(flat[k], low[:, :]).then_inc(cleared, 16)
                sp.dma_start(m[P * C:P * C + P, :], low[:, 0:H]).then_inc(cleared, 16)
            sp.wait_ge(cleared, 32 * T)
            sp.wait_ge(written, steps * 16 * T)
            sp.dma_start(merged[:, :], flat[0]).then_inc(lots, 16)
            for k in range(1, T):
                if k > 1:
                    sp.wait_ge(merging, k - 1)
                sp.dma_start(lot[:, k % 2, :], flat[k]).then_inc(lots, 16)
                sp.wait_ge(lots, 16 * (k + 1))
            sp.wait_ge(merging, T - 1)
            sp.dma_start(flat[0], merged[:, :]).then_inc(final, 16)
            sp.wait_ge(final, 16)

        @block.scalar
        def _(act):
            for slot in slots(act, steps, 0):
                if st := slot.step(0):
                    q = st.ring(2)
                    if st.has(2):
                        act.wait_ge(written, st.count(16 * T, back=2))
                    act.activation(ids[:, q, :], g["dst_f"][:, st.tiles()], ACT.Copy)
                    act.activation(target[:, q, :], g["dst_target"][:, st.tiles()], ACT.Copy)
                    act.activation(own[:, q, :], g["dst_i"][:, st.tiles()], ACT.Copy)
                    act.activation(scores[:, q].rearrange("p t h -> p (t h)"), g["scores"][:, st.tiles(H)],
                                   ACT.Copy).then_inc(staged, 1)

        @block.tensor
        def _(pe):
            for slot in slots(pe, steps, 1):
                if st := slot.step(1):
                    q = st.ring(2)
                    pe.wait_ge(staged, st.count())
                    if st.has(1):
                        pe.wait_ge(masked_ready, st.count(back=1))
                    for t in range(T):
                        pe.matmul(id_rows[:, t, :], ids[:, q, t:t + 1].to_broadcast([P, P]), g["ident"][:, :],
                                  start=True, stop=True)
                        for h in range(H):
                            last = pe.matmul(score_rows[:, t * H + h, :], scores[:, q, t, h:h + 1].to_broadcast([P, P]),
                                             g["ident"][:, :], start=True, stop=True)
                    last.then_inc(spread, 1)

        @block.vector
        def _(dve):
            dve.memset(low[:, :], -FAR).then_inc(low_ready, 1)
            for slot in slots(dve, steps, 3):
                if st := slot.step(3):
                    q = st.ring(2)
                    dve.wait_ge(read, st.count(16 * T))
                    dve.wait_ge(best_ready, st.count())
                    dve.tensor_tensor(new[:, q], seen[:, q], best[:, q], ALU.max).then_inc(renewed, 1)
                if st := slot.step(2):
                    q = st.ring(2)
                    dve.wait_ge(spread, st.count())
                    dve.tensor_tensor(away[:, q], id_rows[:, :, :], ids[:, q].unsqueeze(2).to_broadcast([P, T, P]),
                                      ALU.is_equal).then_inc(same_ready, 1)
                    dve.wait_ge(same_ready, st.count())
                    dve.tensor_scalar(away[:, q], away[:, q], -1.0, FAR, ALU.add, ALU.mult).then_inc(away_ready, 1)
                    dve.wait_ge(away_ready, st.count())
                    for t in range(T):
                        last = dve.tensor_tensor(masked[:, q, t * H:(t + 1) * H, :], score_rows[:, t * H:(t + 1) * H, :],
                                                 away[:, q, t, :].unsqueeze(1).to_broadcast([P, H, P]), ALU.add)
                    last.then_inc(masked_ready, 1)
                    dve.wait_ge(masked_ready, st.count())
                    dve.tensor_reduce(best[:, q].rearrange("p t h -> p (t h)"), masked[:, q], AX.X, ALU.max
                                      ).then_inc(best_ready, 1)
            for k in range(1, T):
                dve.wait_ge(lots, 16 * (k + 1))
                dve.tensor_tensor(merged[:, :], merged[:, :], lot[:, k % 2, :], ALU.max).then_inc(merging, 1)
                dve.wait_ge(merging, k)

        @block.gpsimd
        def _(pool):
            pool.wait_ge(cleared, 32 * T)
            for slot in slots(pool, steps, 3):
                if st := slot.step(3):
                    q = st.ring(2)
                    pool.wait_ge(staged, st.count())
                    if st.has(1):
                        pool.wait_ge(written, st.count(16 * T, back=1))
                    if st.has(2):
                        pool.wait_ge(renewed, st.count(back=2))
                    apart(pool, st, g["passed"])
                    for t in range(T):
                        pool.indirect_dma_start(
                            out=seen[:, q, t, :], out_offset=None, in_=g["max_tables"][t],
                            in_offset=bass.IndirectOffsetOnAxis(own[:, q, t:t + 1], 0)).then_inc(read, 16)
                    pool.wait_ge(renewed, st.count())
                    apart(pool, st, g["passed"])
                    for t in range(T):
                        pool.indirect_dma_start(
                            out=g["max_tables"][t], out_offset=bass.IndirectOffsetOnAxis(target[:, q, t:t + 1], 0),
                            in_=new[:, q, t, :], in_offset=None).then_inc(written, 16)
            pool.wait_ge(read, steps * 16 * T)
            pool.wait_ge(written, steps * 16 * T)


def edge_exp(nc, g, C):
    steps, H = C // T, HEADS
    moved = 16 * T
    with ExitStack() as ctx:
        s = Scope(nc, ctx, "exp")
        own, seen = s.sb("own", [P, R, T], I32), s.sb("seen", [P, R, T * H])
        staged, fetched, less, done = s.sem("staged"), s.sems("fetched"), s.sem("less"), s.sem("done")
        block = s.block()

        @block.gpsimd
        def _(pool):
            for slot in slots(pool, steps, 1):
                if st := slot.step(1):
                    r = st.ring()
                    if st.has(R):
                        pool.wait_ge(less, st.count(back=R))
                    pool.wait_ge(staged, st.count())
                    apart(pool, st, g["passed"])
                    for t in range(T):
                        pool.indirect_dma_start(
                            out=seen[:, r, t * H:(t + 1) * H], out_offset=None, in_=g["max_tables"][0],
                            in_offset=bass.IndirectOffsetOnAxis(own[:, r, t:t + 1], 0)).then_inc(fetched[r], 16)
            all_landed(pool, fetched, steps, moved)

        @block.vector
        def _(dve):
            for slot in slots(dve, steps, 2):
                if st := slot.step(2):
                    r = st.ring()
                    dve.wait_ge(fetched[r], st.landed(moved))
                    dve.tensor_tensor(g["exps"][:, st.tiles(H)], g["scores"][:, st.tiles(H)], seen[:, r, :],
                                      ALU.subtract).then_inc(less, 1)

        @block.scalar
        def _(act):
            for slot in slots(act, steps, 0):
                if st := slot.step(0):
                    if st.has(R):
                        act.wait_ge(fetched[st.ring()], st.landed(moved, back=R))
                    act.activation(own[:, st.ring(), :], g["dst_i"][:, st.tiles()], ACT.Copy).then_inc(staged, 1)
            act.wait_ge(less, steps)
            act.activation(g["exps"][:, :], g["exps"][:, :], ACT.Exp).then_inc(done, 1)
            act.wait_ge(done, 1)


def node_attn(nc, g, C):
    steps, H, W = C // T, HEADS, P + HEADS
    with ExitStack() as ctx:
        s = Scope(nc, ctx, "attn")
        a, b = s.sb("a", [P, R, T, W]), s.sb("b", [P, R, T, W])
        x, h, v, z, zn, base, x3, h3 = (s.sb(k, [P, R, T, P]) for k in ("x", "h", "v", "z", "zn", "base", "x3", "h3"))
        biased = s.sb("biased", [P, 2, T, P])
        den, inv = s.sb("den", [P, 2, T * H]), s.sb("inv", [P, 2, T * H])
        vT = s.sb("vT", [P, 2, T, P])
        vT_ps, product_ps = s.ps("vT_ps", [P, 2, T, P]), s.ps("product_ps", [P, 2, T, P])
        a_landed, b_landed, x_landed, h_landed = (s.sems(k + "_landed") for k in "abxh")
        x3_stored, h3_stored = s.sems("x3_stored"), s.sems("h3_stored")
        agg_ready, den_ready, inv_ready, divided, v_ready, turned, vT_ready, product = (s.sem(k) for k in (
            "agg_ready", "den_ready", "inv_ready", "divided", "v_ready", "turned", "vT_ready", "product"))
        biased_ready, z_ready, gammaed, base_ready, x3_ready = (s.sem(k) for k in (
            "biased_ready", "z_ready", "gammaed", "base_ready", "x3_ready"))
        norm1, norm2 = (Norm(s, k, g["minus_half"], g["passed"]) for k in ("ln1", "ln2"))
        tables = [table_rows(t, C) for t in g["agg_attn"]]
        block = s.block()

        @block.sync
        def _(sp):
            for slot in slots(sp, steps, 9):
                if st := slot.step(9):
                    sp.wait_ge(norm2.normed, st.count())
                    sp.dma_start(rows(g["h3"])[:, st.tiles(), :], h3[:, st.ring()]).then_inc(h3_stored[st.ring()], 16)
                if st := slot.step(8):
                    sp.wait_ge(x3_ready, st.count())
                    sp.dma_start(rows(g["x3"])[:, st.tiles(), :], x3[:, st.ring()]).then_inc(x3_stored[st.ring()], 16)
                if st := slot.step(4):
                    if st.has(R):
                        sp.wait_ge(base_ready, st.count(back=R))
                    sp.dma_start(x[:, st.ring()], rows(g["x2"])[:, st.tiles(), :]).then_inc(x_landed[st.ring()], 16)
                if st := slot.step(0):
                    r = st.ring()
                    if st.has(R):
                        sp.wait_ge(v_ready, st.count(back=R))
                    sp.dma_start(a[:, r], tables[0][:, st.tiles(), :]).then_inc(a_landed[r], 16)
                    sp.dma_start(b[:, r], tables[1][:, st.tiles(), :]).then_inc(b_landed[r], 16)
                    sp.dma_start(h[:, r], rows(g["h2"])[:, st.tiles(), :]).then_inc(h_landed[r], 16)
            for stored in (x3_stored, h3_stored):
                all_landed(sp, stored, steps, 16)

        @block.vector
        def _(dve):
            for slot in slots(dve, steps, 8):
                if st := slot.step(8):
                    norm2.shift(dve, st)
                if st := slot.step(7):
                    r = st.ring()
                    dve.wait_ge(norm1.normed, st.count())
                    dve.tensor_tensor(zn[:, r], zn[:, r], over(g["gamma_attn"]), ALU.mult).then_inc(gammaed, 1)
                    dve.wait_ge(gammaed, st.count())
                    dve.wait_ge(base_ready, st.count())
                    if st.has(R):
                        dve.wait_ge(x3_stored[r], st.landed(16, back=R))
                        dve.wait_ge(norm2.normed, st.count(back=R))
                    dve.tensor_tensor(x3[:, r], zn[:, r], base[:, r], ALU.add).then_inc(x3_ready, 1)
                    dve.wait_ge(x3_ready, st.count())
                    norm2.statistics(dve, st, x3)
                if st := slot.step(6):
                    norm1.shift(dve, st)
                if st := slot.step(5):
                    dve.wait_ge(z_ready, st.count())
                    norm1.statistics(dve, st, z)
                if st := slot.step(4):
                    q = st.ring(2)
                    dve.wait_ge(product, st.count())
                    if st.has(2):
                        dve.wait_ge(z_ready, st.count(back=2))
                    dve.tensor_tensor(biased[:, q], product_ps[:, q], over(g["b_out"]), ALU.add).then_inc(biased_ready, 1)
                if st := slot.step(1):
                    r, q = st.ring(), st.ring(2)
                    dve.wait_ge(a_landed[r], st.landed(16))
                    dve.wait_ge(b_landed[r], st.landed(16))
                    dve.tensor_tensor(a[:, r], a[:, r], b[:, r], ALU.add).then_inc(agg_ready, 1)
                    dve.wait_ge(agg_ready, st.count())
                    dve.tensor_scalar(den[:, q].rearrange("p (t h) -> p t h", h=H), a[:, r, :, P:W], 1.0, None,
                                      ALU.max).then_inc(den_ready, 1)
                    dve.wait_ge(den_ready, st.count())
                    dve.reciprocal(inv[:, q], den[:, q]).then_inc(inv_ready, 1)
                    dve.wait_ge(inv_ready, st.count())
                    if st.has(R):
                        dve.wait_ge(turned, st.count(back=R))
                    for t in range(T):
                        last = dve.tensor_tensor(v[:, r, t].rearrange("p (h d) -> p h d", h=H),
                                                 a[:, r, t, 0:P].rearrange("p (h d) -> p h d", h=H),
                                                 inv[:, q, t * H:(t + 1) * H].unsqueeze(2).to_broadcast([P, H, P // H]),
                                                 ALU.mult)
                    last.then_inc(divided, 1)

        @block.gpsimd
        def _(pool):
            for slot in slots(pool, steps, 7):
                if st := slot.step(7):
                    norm2.power(pool, st)
                if st := slot.step(6):
                    r = st.ring()
                    if st.has(R):
                        pool.wait_ge(x3_ready, st.count(back=R))
                    pool.wait_ge(x_landed[r], st.landed(16))
                    pool.tensor_tensor(base[:, r], x[:, r], over(g["beta_attn"]), ALU.add).then_inc(base_ready, 1)
                if st := slot.step(5):
                    norm1.power(pool, st)
                if st := slot.step(1):
                    r = st.ring()
                    pool.wait_ge(h_landed[r], st.landed(16))
                    pool.wait_ge(divided, st.count())
                    pool.tensor_tensor(v[:, r], v[:, r], h[:, r], ALU.add).then_inc(v_ready, 1)

        @block.scalar
        def _(act):
            for slot in slots(act, steps, 8):
                if st := slot.step(8):
                    if st.has(R):
                        act.wait_ge(h3_stored[st.ring()], st.landed(16, back=R))
                    norm2.apply(act, st, h3, x3, ACT.Relu)
                if st := slot.step(6):
                    if st.has(R):
                        act.wait_ge(x3_ready, st.count(back=R))
                    norm1.apply(act, st, zn, z, ACT.Identity)
                if st := slot.step(4):
                    act.wait_ge(biased_ready, st.count())
                    if st.has(R):
                        act.wait_ge(norm1.normed, st.count(back=R))
                    act.activation(z[:, st.ring()], biased[:, st.ring(2)], ACT.Relu).then_inc(z_ready, 1)
                if st := slot.step(2):
                    act.wait_ge(turned, st.count())
                    if st.has(2):
                        act.wait_ge(product, st.count(back=2))
                    act.activation(vT[:, st.ring(2)], vT_ps[:, st.ring(2)], ACT.Copy).then_inc(vT_ready, 1)

        @block.tensor
        def _(pe):
            for slot in slots(pe, steps, 3):
                if st := slot.step(3):
                    q = st.ring(2)
                    pe.wait_ge(vT_ready, st.count())
                    if st.has(2):
                        pe.wait_ge(biased_ready, st.count(back=2))
                    for t in range(T):
                        last = pe.matmul(product_ps[:, q, t, :], vT[:, q, t, :], g["w_out"][:, :], start=True, stop=True)
                    last.then_inc(product, 1)
                if st := slot.step(2):
                    pe.wait_ge(v_ready, st.count())
                    if st.has(2):
                        pe.wait_ge(vT_ready, st.count(back=2))
                    for t in range(T):
                        last = pe.transpose(vT_ps[:, st.ring(2), t, :], v[:, st.ring(), t, :], g["ident"][:, :])
                    last.then_inc(turned, 1)


def node_sage(nc, g, C):
    steps, W = C // T, P + 1
    with ExitStack() as ctx:
        s = Scope(nc, ctx, "sage")
        a, b = s.sb("a", [P, R, T, W]), s.sb("b", [P, R, T, W])
        x, h, mean, g4, r4 = (s.sb(k, [P, R, T, P]) for k in ("x", "h", "mean", "g4", "r4"))
        inT, hid = s.sb("inT", [P, 2, 2, T * P]), s.sb("hid", [P, 2, 2, T * P])
        count, inv = s.sb("count", [P, 2, T]), s.sb("inv", [P, 2, T])
        mT_ps, hT_ps, hid_ps = s.ps("mT_ps", [P, T, P]), s.ps("hT_ps", [P, T, P]), s.ps("hid_ps", [P, 2, T * P])
        g4_ps, r4_ps = s.ps("g4_ps", [P, 2, T, P]), s.ps("r4_ps", [P, 2, T, P])
        a_landed, b_landed, x_landed, h_landed = (s.sems(k + "_landed") for k in "abxh")
        g4_stored, r4_stored = s.sems("g4_stored"), s.sems("r4_stored")
        agg_ready, count_ready, inv_ready, mean_ready, m_turned, h_turned, mT_ready, hT_ready = (s.sem(k) for k in (
            "agg_ready", "count_ready", "inv_ready", "mean_ready", "m_turned", "h_turned", "mT_ready", "hT_ready"))
        hid_product, hid_ready, out_product, g4_ready, base_ready, r4_ready = (s.sem(k) for k in (
            "hid_product", "hid_ready", "out_product", "g4_ready", "base_ready", "r4_ready"))
        tables = [table_rows(t, C) for t in g["agg_sage1"]]
        block = s.block()

        @block.sync
        def _(sp):
            for slot in slots(sp, steps, 5):
                if st := slot.step(5):
                    r = st.ring()
                    sp.wait_ge(g4_ready, st.count())
                    sp.dma_start(rows(g["g4"])[:, st.tiles(), :], g4[:, r]).then_inc(g4_stored[r], 16)
                    sp.wait_ge(r4_ready, st.count())
                    sp.dma_start(rows(g["r4"])[:, st.tiles(), :], r4[:, r]).then_inc(r4_stored[r], 16)
                if st := slot.step(0):
                    r = st.ring()
                    if st.has(R):
                        sp.wait_ge(mean_ready, st.count(back=R))
                        sp.wait_ge(h_turned, st.count(back=R))
                        sp.wait_ge(base_ready, st.count(back=R))
                    sp.dma_start(a[:, r], tables[0][:, st.tiles(), :]).then_inc(a_landed[r], 16)
                    sp.dma_start(b[:, r], tables[1][:, st.tiles(), :]).then_inc(b_landed[r], 16)
                    sp.dma_start(h[:, r], rows(g["h3"])[:, st.tiles(), :]).then_inc(h_landed[r], 16)
                    sp.dma_start(x[:, r], rows(g["x3"])[:, st.tiles(), :]).then_inc(x_landed[r], 16)
            for stored in (g4_stored, r4_stored):
                all_landed(sp, stored, steps, 16)

        @block.vector
        def _(dve):
            for slot in slots(dve, steps, 4):
                if st := slot.step(4):
                    r = st.ring()
                    dve.wait_ge(out_product, st.count())
                    dve.wait_ge(base_ready, st.count())
                    dve.tensor_tensor(r4[:, r], r4[:, r], r4_ps[:, st.ring(2)], ALU.add).then_inc(r4_ready, 1)
                if st := slot.step(1):
                    r, q = st.ring(), st.ring(2)
                    dve.wait_ge(a_landed[r], st.landed(16))
                    dve.wait_ge(b_landed[r], st.landed(16))
                    dve.tensor_tensor(a[:, r], a[:, r], b[:, r], ALU.add).then_inc(agg_ready, 1)
                    dve.wait_ge(agg_ready, st.count())
                    dve.tensor_scalar(count[:, q, :], a[:, r, :, P], 1.0, None, ALU.max).then_inc(count_ready, 1)
                    dve.wait_ge(count_ready, st.count())
                    dve.reciprocal(g["inv_count"][:, st.tiles()], count[:, q, :])
                    dve.reciprocal(inv[:, q, :], count[:, q, :]).then_inc(inv_ready, 1)
                    dve.wait_ge(inv_ready, st.count())
                    if st.has(R):
                        dve.wait_ge(m_turned, st.count(back=R))
                    dve.tensor_tensor(mean[:, r], a[:, r, :, 0:P], inv[:, q, :].unsqueeze(2).to_broadcast([P, T, P]),
                                      ALU.mult).then_inc(mean_ready, 1)

        @block.gpsimd
        def _(pool):
            for slot in slots(pool, steps, 2):
                if st := slot.step(2):
                    r = st.ring()
                    if st.has(R):
                        pool.wait_ge(r4_stored[r], st.landed(16, back=R))
                    pool.wait_ge(x_landed[r], st.landed(16))
                    pool.tensor_tensor(r4[:, r], x[:, r], over(g["b2_sage"]), ALU.add).then_inc(base_ready, 1)

        @block.scalar
        def _(act):
            for slot in slots(act, steps, 4):
                if st := slot.step(4):
                    r = st.ring()
                    act.wait_ge(out_product, st.count())
                    if st.has(R):
                        act.wait_ge(g4_stored[r], st.landed(16, back=R))
                    act.activation(g4[:, r], g4_ps[:, st.ring(2)], ACT.Copy).then_inc(g4_ready, 1)
                if st := slot.step(3):
                    act.wait_ge(hid_product, st.count())
                    if st.has(2):
                        act.wait_ge(out_product, st.count(back=2))
                    for m in range(2):
                        last = act.activation(hid[:, st.ring(2), m, :], hid_ps[:, m, :], ACT.Relu,
                                              bias=g["b1_sage"][:, m:m + 1])
                    last.then_inc(hid_ready, 1)
                if st := slot.step(2):
                    q = st.ring(2)
                    if st.has(2):
                        act.wait_ge(hid_product, st.count(back=2))
                    act.wait_ge(h_turned, st.count())
                    act.activation(inT[:, q, 1, :], hT_ps[:, :, :].rearrange("p t n -> p (t n)"), ACT.Copy).then_inc(hT_ready, 1)
                    act.wait_ge(m_turned, st.count())
                    act.activation(inT[:, q, 0, :], mT_ps[:, :, :].rearrange("p t n -> p (t n)"), ACT.Copy).then_inc(mT_ready, 1)

        @block.tensor
        def _(pe):
            for slot in slots(pe, steps, 4):
                if st := slot.step(4):
                    q = st.ring(2)
                    pe.wait_ge(hid_ready, st.count())
                    if st.has(2):
                        pe.wait_ge(g4_ready, st.count(back=2))
                        pe.wait_ge(r4_ready, st.count(back=2))
                    for half, out in enumerate((g4_ps, r4_ps)):
                        for t in range(T):
                            for m in range(2):
                                last = pe.matmul(out[:, q, t, :], hid[:, q, m, t * P:(t + 1) * P],
                                                 g["w2_sage"][:, m, half * P:(half + 1) * P], start=(m == 0), stop=(m == 1))
                    last.then_inc(out_product, 1)
                if st := slot.step(3):
                    q = st.ring(2)
                    pe.wait_ge(mT_ready, st.count())
                    pe.wait_ge(hT_ready, st.count())
                    if st.has(1):
                        pe.wait_ge(hid_ready, st.count(back=1))
                    for m in range(2):
                        for k in range(2):
                            last = pe.matmul(hid_ps[:, m, :], g["w1_sage"][:, k, m * P:(m + 1) * P], inT[:, q, k, :],
                                             start=(k == 0), stop=(k == 1))
                    last.then_inc(hid_product, 1)
                if st := slot.step(2):
                    r = st.ring()
                    pe.wait_ge(h_landed[r], st.landed(16))
                    if st.has(1):
                        pe.wait_ge(hT_ready, st.count(back=1))
                    for t in range(T):
                        last = pe.transpose(hT_ps[:, t, :], h[:, r, t, :], g["ident"][:, :])
                    last.then_inc(h_turned, 1)
                    pe.wait_ge(mean_ready, st.count())
                    if st.has(1):
                        pe.wait_ge(mT_ready, st.count(back=1))
                    for t in range(T):
                        last = pe.transpose(mT_ps[:, t, :], mean[:, r, t, :], g["ident"][:, :])
                    last.then_inc(m_turned, 1)


def node_out(nc, g, C):
    steps = C // T
    with ExitStack() as ctx:
        s = Scope(nc, ctx, "out")
        a, b, x, y = (s.sb(k, [P, R, T, P]) for k in ("a", "b", "x", "y"))
        inv = s.sb("inv", [P, R, T])
        a_landed, b_landed, x_landed = (s.sems(k + "_landed") for k in "abx")
        staged, agg_ready, scaled, y_ready, y_stored = (
            s.sem("staged"), s.sem("agg_ready"), s.sem("scaled"), s.sem("y_ready"), s.sems("y_stored"))
        tables = [table_rows(t, C) for t in g["agg_sage2"]]
        block = s.block()

        @block.sync
        def _(sp):
            for slot in slots(sp, steps, 3):
                if st := slot.step(3):
                    r = st.ring()
                    sp.wait_ge(y_ready, st.count())
                    sp.dma_start(rows(g["out"])[:, st.tiles(), :], y[:, r]).then_inc(y_stored[r], 16)
                if st := slot.step(0):
                    r = st.ring()
                    if st.has(R):
                        sp.wait_ge(y_ready, st.count(back=R))
                    sp.dma_start(a[:, r], tables[0][:, st.tiles(), :]).then_inc(a_landed[r], 16)
                    sp.dma_start(b[:, r], tables[1][:, st.tiles(), :]).then_inc(b_landed[r], 16)
                    sp.dma_start(x[:, r], rows(g["r4"])[:, st.tiles(), :]).then_inc(x_landed[r], 16)
            all_landed(sp, y_stored, steps, 16)

        @block.vector
        def _(dve):
            for slot in slots(dve, steps, 2):
                if st := slot.step(2):
                    r = st.ring()
                    dve.wait_ge(scaled, st.count())
                    dve.wait_ge(x_landed[r], st.landed(16))
                    dve.tensor_tensor(y[:, r], y[:, r], x[:, r], ALU.add).then_inc(y_ready, 1)
                if st := slot.step(1):
                    r = st.ring()
                    dve.wait_ge(a_landed[r], st.landed(16))
                    dve.wait_ge(b_landed[r], st.landed(16))
                    dve.tensor_tensor(a[:, r], a[:, r], b[:, r], ALU.add).then_inc(agg_ready, 1)

        @block.scalar
        def _(act):
            for slot in slots(act, steps, 1):
                if st := slot.step(1):
                    r = st.ring()
                    act.wait_ge(staged, st.count())
                    act.wait_ge(agg_ready, st.count())
                    if st.has(R):
                        act.wait_ge(y_stored[r], st.landed(16, back=R))
                    for t in range(T):
                        last = act.activation(y[:, r, t, :], a[:, r, t, :], ACT.Copy, scale=inv[:, r, t:t + 1])
                    last.then_inc(scaled, 1)
                if st := slot.step(0):
                    r = st.ring()
                    if st.has(R):
                        act.wait_ge(scaled, st.count(back=R))
                    act.activation(inv[:, r, :], g["inv_count"][:, st.tiles()], ACT.Copy).then_inc(staged, 1)


def build(nc, g, C):
    N = P * C
    with ExitStack() as ctx:
        def sb(name, shape, dt=F32):
            g[name] = ctx.enter_context(nc.sbuf_tensor(name, shape, dt))
            return g[name]

        def dram(name, shape):
            return nc.dram_tensor(name, shape, F32, kind="Internal").ap()

        for name in ("h0", "h1", "xh", "x2", "h2", "y2", "xp", "x3", "h3", "g4", "r4"):
            g[name] = dram("rows_" + name, (N, P))
        for name, width in (("rel", P), ("mlp", P), ("attn", P + HEADS), ("sage1", P + 1), ("sage2", P)):
            g["agg_" + name] = [dram(f"agg_{name}{k}", (N + P, width)) for k in range(TABLES)]
        g["max_tables"] = [dram(f"maxima{t}", (N + P, HEADS)) for t in range(T)]

        for key in ("src", "dst"):
            sb(key + "_i", [P, C], I32)
            for form in ("_f", "_spare", "_target"):
                sb(key + form, [P, C])
        sb("weight", [P, C])
        sb("scores", [P, C * HEADS])
        sb("exps", [P, C * HEADS])
        sb("inv_count", [P, C])
        sb("ident", [P, P])
        sb("before", [P, P])
        sb("ones", [P, 1])
        sb("minus_half", [P, T])
        sb("spare_i", [P, 1], I32)
        sb("spare_f", [P, 1])
        sb("zeros", [P, T * (P + HEADS)])
        sb("unsorted_i", [P, 1], I32)
        g["unsorted"] = nc.dram_tensor("unsorted", (1, 1), I32, kind="Internal").ap()
        loads = []

        def const(name, shape, dram_ap):
            sb(name, shape)
            loads.append((g[name][:], dram_ap))

        const("w_rel", [P, P], g["L0_w"])
        const("w1_mlp", [P, 2, 2 * P], g["L1_gnn_W1"].rearrange("(k p) n -> p k n", p=P))
        const("w2_mlp", [P, 2, P], g["L1_gnn_W2"].rearrange("(k p) n -> p k n", p=P))
        const("b1_mlp", [P, 2], g["L1_b1"])
        E = g["edge_attr_64"].shape[1]
        const("w_node", [P, P], g["L2_w_proj"][0:P, :])
        const("w_edge", [E, P], g["L2_w_proj"][P:P + E, :])
        const("w_out", [P, P], g["L2_w_out"])
        sb("w1_sage", [P, 2, 2 * P])
        sb("w2_sage", [P, 2, 2 * P])
        for k, half in enumerate(("l", "r")):
            loads.append((g["w1_sage"][:, k, :], g["L3_gnn_W1_" + half]))
            loads.append((g["w2_sage"][:, :, k * P:(k + 1) * P], g["L3_gnn_W2_" + half].rearrange("(k p) n -> p k n", p=P)))
        const("b1_sage", [P, 2], g["L3_b1"])
        for name, key in (("b2_mlp", "L1_gnn_b2"), ("gamma_mlp", "L1_gnn_ln_gamma"), ("beta_mlp", "L1_gnn_ln_beta"),
                          ("b_proj", "L2_gnn_W_proj_b"), ("attn", "L2_attn"), ("b_out", "L2_gnn_W_out_b"),
                          ("gamma_attn", "L2_gnn_ln_gamma"), ("beta_attn", "L2_gnn_ln_beta"), ("b2_sage", "L3_gnn_b2")):
            const(name, [P, P], g[key].rearrange("(o n) -> o n", o=1).to_broadcast([P, P]))
        g["loads"] = loads

        g["passed"] = ctx.enter_context(nc.semaphore("passed"))
        setup(nc, g, C)
        node_norm(nc, g, C, zero=g["agg_rel"])
        edge_sum(nc, g, C, "rel_sum", g["agg_rel"], "src", gather=(g["h0"], g["dst_i"]), weighted=True, first=True,
                 zero=g["agg_mlp"])
        node_rel(nc, g, C, zero=g["agg_attn"])
        edge_sum(nc, g, C, "mlp_sum", g["agg_mlp"], "dst", load=g["edge_attr_128"], first=True, zero=g["agg_sage1"])
        node_mlp(nc, g, C)
        edge_project(nc, g, C)
        unsorted = nc.values_load(g["unsorted"])
        with nc.If(unsorted == 0):
            edge_exp_sorted(nc, g, C)
        with nc.Else():
            edge_max(nc, g, C)
            edge_exp(nc, g, C)
        edge_sum(nc, g, C, "attn_sum", g["agg_attn"], "dst", load=g["xp"], extra="exp", zero=g["agg_sage2"])
        node_attn(nc, g, C)
        edge_sum(nc, g, C, "sage1_sum", g["agg_sage1"], "dst", gather=(g["h3"], g["src_i"]), extra="ones")
        node_sage(nc, g, C)
        edge_sum(nc, g, C, "sage2_sum", g["agg_sage2"], "dst", gather=(g["g4"], g["src_i"]))
        node_out(nc, g, C)


def kernel(**inputs):
    import concourse.bacc as bacc
    from concourse.bass_utils import run_bass_kernel_spmd

    nodes, D = inputs["x"].shape
    edges = inputs["src"].shape[0]
    C = -(-(max(nodes, edges) + 1) // (P * T)) * T

    def padded(a, value=0):
        a = np.asarray(a)
        return np.concatenate([a, np.full((P * C - a.shape[0],) + a.shape[1:], value, a.dtype)])

    halves = lambda b: np.ascontiguousarray(np.asarray(b).reshape(2, P).T)
    arrays = {
        "x": padded(inputs["x"]),
        "src": padded(inputs["src"], nodes),
        "dst": padded(inputs["dst"], nodes),
        "edge_weight": padded(inputs["edge_weight"]),
        "edge_attr_128": padded(inputs["edge_attr_128"]),
        "edge_attr_64": padded(inputs["edge_attr_64"]),
        "L0_w": np.ascontiguousarray(np.asarray(inputs["L0_gnn_weights"])[0].T),
        "L1_b1": halves(inputs["L1_gnn_b1"]),
        "L2_w_proj": np.ascontiguousarray(np.asarray(inputs["L2_gnn_W_proj_w"]).T),
        "L2_w_out": np.ascontiguousarray(np.asarray(inputs["L2_gnn_W_out_w"]).T),
        "L2_attn": np.asarray(inputs["L2_gnn_attn_vec"]).reshape(-1),
        "L3_b1": halves(inputs["L3_gnn_b1"]),
    }
    for name in ("L1_gnn_W1", "L1_gnn_W2", "L1_gnn_b2", "L1_gnn_ln_gamma", "L1_gnn_ln_beta", "L2_gnn_W_proj_b",
                 "L2_gnn_W_out_b", "L2_gnn_ln_gamma", "L2_gnn_ln_beta", "L3_gnn_W1_l", "L3_gnn_W1_r",
                 "L3_gnn_W2_l", "L3_gnn_W2_r", "L3_gnn_b2"):
        arrays[name] = np.ascontiguousarray(inputs[name])
    nc = bacc.Bacc("TRN2", target_bir_lowering=False, num_devices=1)
    g = {name: nc.dram_tensor(name, a.shape, mybir.dt.from_np(a.dtype), kind="ExternalInput").ap()
         for name, a in arrays.items()}
    g["out"] = nc.dram_tensor("out", (P * C, D), F32, kind="ExternalOutput").ap()
    build(nc, g, C)
    result = run_bass_kernel_spmd(nc, [arrays], core_ids=[0])
    return result.results[0]["out"][:nodes]
```

```python
from contextlib import ExitStack

import numpy as np

import concourse.bass as bass
from concourse import mybir

P = 128
T = 4
R = 4
EPS = 1e-5
TABLES = 2
HEADS = 4
FAR = 1e30

F32 = mybir.dt.float32
I32 = mybir.dt.int32
ALU = mybir.AluOpType
ACT = mybir.ActivationFunctionType
AX = mybir.AxisListType


class Step:

    def __init__(self, i, b):
        self.i, self.b = i, b
        self.static = isinstance(i, int)
        self.n = i * R + b

    def has(self, back):
        return not self.static or self.b >= back

    def ring(self, depth=R):
        return self.b % depth

    def count(self, per_step=1, back=0):
        return self.i * (R * per_step) + (self.b + 1 - back) * per_step

    def landed(self, per_step=1, back=0):
        return self.i * per_step + ((self.b - back) // R + 1) * per_step

    def tiles(self, width=1):
        return bass.ds(self.i * (R * T * width) + self.b * T * width, T * width)


def slots(eng, steps, most):
    first = most + R
    rounds = max((steps - first) // R, 0)
    for u in range(min(first, steps + most)):
        yield Slot(0, u, steps)
    if rounds:
        with eng.Fori(0, rounds) as i:
            for k in range(R):
                yield Slot(i, first + k, steps)
    for u in range(first + rounds * R, steps + most):
        yield Slot(0, u, steps)


class Slot:
    def __init__(self, i, u, steps):
        self.i, self.u, self.steps = i, u, steps

    def step(self, lag):
        if isinstance(self.i, int) and not 0 <= self.u - lag < self.steps:
            return None
        return Step(self.i, self.u - lag)


class Scope:

    def __init__(self, nc, ctx, name):
        self.nc, self.ctx, self.name, self.all_sems = nc, ctx, name, []

    def sb(self, name, shape, dt=F32):
        return self.ctx.enter_context(self.nc.sbuf_tensor(f"{self.name}_{name}", shape, dt))

    def ps(self, name, shape):
        return self.ctx.enter_context(self.nc.psum_tensor(f"{self.name}_{name}", shape, F32))

    def sem(self, name):
        self.all_sems.append(self.ctx.enter_context(self.nc.semaphore(f"{self.name}_{name}")))
        return self.all_sems[-1]

    def sems(self, name, n=R):
        return [self.sem(f"{name}{k}") for k in range(n)]

    def block(self):
        self.nc.gpsimd.dma_reset()
        for sem in self.all_sems:
            self.nc.gpsimd.sem_clear(sem)
        self.nc.all_engine_barrier()
        return self.ctx.enter_context(self.nc.Block())


def rows(table):
    return table.rearrange("(p c) d -> p c d", p=P)


def table_rows(table, C):
    return rows(table[0:P * C, :])


def all_landed(eng, sems, steps, per_step):
    for k, sem in enumerate(sems):
        if k < steps:
            eng.wait_ge(sem, len(range(k, steps, R)) * per_step)


def hidden(table, st):
    return table[:, bass.ds(st.i * (R * 2 * T * P) + st.b * 2 * T * P, 2 * T * P)]


def over(vector):
    return vector[:, :].unsqueeze(1).to_broadcast([P, T, P])


def apart(eng, st, passed):
    if not st.static:
        eng.sem_inc(passed, 1)


def zero_step(sp, g, C, tables, st, zeroed, beside=None):
    for k, table in enumerate(tables):
        if beside:
            beside.pace(sp, st, k * T // len(tables))
        W = table.shape[1]
        sp.dma_start(table_rows(table, C)[:, st.tiles(), :],
                     g["zeros"][:, 0:T * W].rearrange("p (t w) -> p t w", t=T)).then_inc(zeroed, 16)


def zero_spare(sp, g, C, tables, zeroed):
    for table in tables:
        sp.dma_start(table[P * C:P * C + P, :], g["zeros"][:, 0:table.shape[1]]).then_inc(zeroed, 16)


def zeroings(tables, steps):
    return 16 * len(tables) * (steps + 1)


def setup(nc, g, C):
    with ExitStack() as ctx:
        s = Scope(nc, ctx, "setup")
        last_first = s.sb("last_first", [P, 2])
        falls, fall = s.sb("falls", [P, C]), s.sb("fall", [P, 2])
        edge_ids, cross, total = s.sb("edge_ids", [1, 2, P]), s.sb("cross", [1, P]), s.sb("total", [1, 4])
        ids_row, fall_sum = s.ps("ids_row", [1, 2, P]), s.ps("fall_sum", [1, 1])
        loaded, made, chain = s.sem("loaded"), s.sem("made"), s.sem("chain")
        spare_ready, constants, turned = s.sem("spare_ready"), s.sem("constants"), s.sem("turned")
        copied, kept = s.sem("copied"), s.sem("kept")
        loads = [(g["src_i"][:, :], g["src"].rearrange("(p c) -> p c", p=P)),
                 (g["dst_i"][:, :], g["dst"].rearrange("(p c) -> p c", p=P)),
                 (g["weight"][:, :], g["edge_weight"].rearrange("(p c) -> p c", p=P))] + g["loads"]
        block = s.block()

        @block.sync
        def _(sp):
            for out, in_ in loads:
                sp.dma_start(out, in_).then_inc(loaded, 16)
            sp.wait_ge(loaded, 16 * len(loads))
            sp.wait_ge(copied, 8)
            sp.dma_start(g["unsorted"], g["unsorted_i"][0:1, 0:1]).then_inc(kept, 16)
            sp.wait_ge(kept, 16)

        @block.gpsimd
        def _(pool):
            pool.memset(g["ident"][:, :], 0.0).then_inc(made, 1)
            pool.memset(g["before"][:, :], 1.0).then_inc(made, 1)
            pool.memset(g["ones"][:, :], 1.0)
            pool.memset(g["ones_row"][:, :], 1.0)
            pool.memset(g["zeros"][:, :], 0.0)
            pool.memset(g["minus_half"][:, :], -0.5)
            pool.iota(g["spare_i"][:, :], [[0, 1]], base=P * C, channel_multiplier=1).then_inc(spare_ready, 1)
            pool.wait_ge(made, 2)
            pool.affine_select(out=g["ident"][:, :], in_=g["ident"][:, :], compare_op=ALU.not_equal,
                               fill=1.0, base=0, pattern=[[-1, P]], channel_multiplier=1)
            pool.affine_select(out=g["before"][:, :], in_=g["before"][:, :], compare_op=ALU.is_gt,
                               fill=0.0, base=0, pattern=[[-1, P]], channel_multiplier=1).then_inc(constants, 1)

        @block.vector
        def _(dve):
            dve.wait_ge(loaded, 16 * len(loads))
            dve.wait_ge(spare_ready, 1)
            dve.tensor_copy(g["src_f"][:, :], g["src_i"][:, :])
            dve.tensor_copy(g["dst_f"][:, :], g["dst_i"][:, :])
            dve.tensor_copy(g["spare_f"][:, :], g["spare_i"][:, :]).then_inc(chain, 1)
            dve.wait_ge(chain, 1)
            for key in ("src", "dst"):
                dve.tensor_scalar(g[key + "_spare"][:, :], g[key + "_f"][:, :], -1.0, g["spare_f"][:, 0:1],
                                  ALU.mult, ALU.add)
            dve.tensor_copy(last_first[:, 0:1], g["dst_f"][:, C - 1:C])
            dve.tensor_copy(last_first[:, 1:2], g["dst_f"][:, 0:1]).then_inc(copied, 1)
            dve.tensor_tensor(falls[:, 0:C - 1], g["dst_f"][:, 0:C - 1], g["dst_f"][:, 1:C],
                              ALU.is_gt).then_inc(copied, 1)
            dve.wait_ge(copied, 2)
            dve.tensor_reduce(fall[:, 0:1], falls[:, 0:C - 1], AX.X, ALU.add).then_inc(copied, 1)
            dve.wait_ge(turned, 1)
            dve.tensor_copy(edge_ids[:, :, :], ids_row[:, :, :]).then_inc(copied, 1)
            dve.wait_ge(copied, 4)
            dve.tensor_tensor(cross[:, 0:P - 1], edge_ids[:, 0, 0:P - 1], edge_ids[:, 1, 1:P], ALU.is_gt).then_inc(copied, 1)
            dve.wait_ge(copied, 5)
            dve.tensor_reduce(total[:, 0:1], cross[:, 0:P - 1], AX.X, ALU.add).then_inc(copied, 1)
            dve.wait_ge(copied, 6)
            dve.wait_ge(turned, 2)
            dve.tensor_tensor(total[:, 1:2], total[:, 0:1], fall_sum[:, :], ALU.add).then_inc(copied, 1)
            dve.wait_ge(copied, 7)
            dve.tensor_scalar(g["unsorted_i"][0:1, 0:1], total[:, 1:2], 1.0, None, ALU.min).then_inc(copied, 1)

        @block.tensor
        def _(pe):
            pe.wait_ge(constants, 1)
            pe.wait_ge(copied, 1)
            for k in range(2):
                last = pe.transpose(ids_row[:, k, :], last_first[:, k:k + 1], g["ident"][:, :])
            last.then_inc(turned, 1)
            pe.wait_ge(copied, 3)
            pe.matmul(fall_sum[:, :], fall[:, 0:1], g["ones"][:, 0:1], start=True, stop=True).then_inc(turned, 1)


class Norm:

    def __init__(self, s, name, minus_half, passed):
        self.minus_half, self.passed = minus_half, passed
        self.stats = s.sb(name + "_stats", [P, 2, T, 6])
        self.moments = s.sb(name + "_moments", [P, R, T, 2])
        self.var, self.rstd, self.offset = (s.sb(f"{name}_{n}", [P, R, T]) for n in ("var", "rstd", "offset"))
        self.stats_ready, self.moments_ready = s.sem(name + "_stats_ready"), s.sem(name + "_moments_ready")
        self.var_ready, self.rstd_ready = s.sem(name + "_var_ready"), s.sem(name + "_rstd_ready")
        self.offset_ready, self.normed = s.sem(name + "_offset_ready"), s.sem(name + "_normed")

    def statistics(self, dve, st, x):
        r, q = st.ring(), st.ring(2)
        for t in range(T):
            last = dve.bn_stats(self.stats[:, q, t, :], x[:, r, t, :])
        last.then_inc(self.stats_ready, 1)

    def aggregate(self, dve, st):
        r, q = st.ring(), st.ring(2)
        if st.has(R):
            dve.wait_ge(self.offset_ready, st.count(back=R))
        dve.wait_ge(self.stats_ready, st.count())
        apart(dve, st, self.passed)
        for t in range(T):
            last = dve.bn_aggr(self.moments[:, r, t, :], self.stats[:, q, t, :])
        last.then_inc(self.moments_ready, 1)

    def power(self, pool, st):
        r = st.ring()
        if st.has(R):
            pool.wait_ge(self.normed, st.count(back=R))
        pool.wait_ge(self.moments_ready, st.count())
        apart(pool, st, self.passed)
        pool.tensor_scalar(self.var[:, r, :], self.moments[:, r, :, 1], EPS, None, ALU.add).then_inc(self.var_ready, 1)
        pool.wait_ge(self.var_ready, st.count())
        pool.tensor_tensor(self.rstd[:, r, :], self.var[:, r, :], self.minus_half[:, 0:T],
                           ALU.pow).then_inc(self.rstd_ready, 1)

    def shift(self, dve, st):
        r = st.ring()
        if st.has(R):
            dve.wait_ge(self.normed, st.count(back=R))
        dve.wait_ge(self.rstd_ready, st.count())
        dve.scalar_tensor_tensor(out=self.offset[:, r, :], in0=self.moments[:, r, :, 0], scalar=-1.0,
                                 in1=self.rstd[:, r, :], op0=ALU.mult, op1=ALU.mult).then_inc(self.offset_ready, 1)

    def apply(self, act, st, out, x, func):
        r = st.ring()
        act.wait_ge(self.offset_ready, st.count())
        for t in range(T):
            last = act.activation(out[:, r, t, :], x[:, r, t, :], func, bias=self.offset[:, r, t:t + 1],
                                  scale=self.rstd[:, r, t:t + 1])
        last.then_inc(self.normed, 1)


def node_norm(nc, g, C, zero):
    steps = C // T
    with ExitStack() as ctx:
        s = Scope(nc, ctx, "norm")
        x, h, y = (s.sb(k, [P, R, T, P]) for k in ("x", "h", "y"))
        hT = s.sb("hT", [P, 2, T, P])
        hT_ps, product_ps = s.ps("hT_ps", [P, 2, T, P]), s.ps("product_ps", [P, 2, T, P])
        x_landed, y_stored, zeroed = s.sems("x_landed"), s.sems("y_stored"), s.sem("zeroed")
        turned, hT_ready, product, y_ready = s.sem("turned"), s.sem("hT_ready"), s.sem("product"), s.sem("y_ready")
        norm = Norm(s, "ln", g["minus_half"], g["passed"])
        block = s.block()

        @block.sync
        def _(sp):
            zero_spare(sp, g, C, zero, zeroed)
            for slot in slots(sp, steps, 7):
                if st := slot.step(7):
                    sp.wait_ge(y_ready, st.count())
                    sp.dma_start(rows(g["y0"])[:, st.tiles(), :], y[:, st.ring()]).then_inc(y_stored[st.ring()], 16)
                if st := slot.step(0):
                    if st.has(R):
                        sp.wait_ge(norm.normed, st.count(back=R))
                    sp.dma_start(x[:, st.ring()], rows(g["x"])[:, st.tiles(), :]).then_inc(x_landed[st.ring()], 16)
                    zero_step(sp, g, C, zero, st, zeroed)
            all_landed(sp, y_stored, steps, 16)
            sp.wait_ge(zeroed, zeroings(zero, steps))

        @block.vector
        def _(dve):
            for slot in slots(dve, steps, 6):
                if st := slot.step(6):
                    dve.wait_ge(product, st.count())
                    if st.has(R):
                        dve.wait_ge(y_stored[st.ring()], st.landed(16, back=R))
                    dve.tensor_copy(y[:, st.ring()], product_ps[:, st.ring(2)]).then_inc(y_ready, 1)
                if st := slot.step(2):
                    norm.shift(dve, st)
                if st := slot.step(1):
                    dve.wait_ge(x_landed[st.ring()], st.landed(16))
                    norm.statistics(dve, st, x)
                    norm.aggregate(dve, st)

        @block.gpsimd
        def _(pool):
            for slot in slots(pool, steps, 1):
                if st := slot.step(1):
                    norm.power(pool, st)

        @block.scalar
        def _(act):
            for slot in slots(act, steps, 4):
                if st := slot.step(4):
                    act.wait_ge(turned, st.count())
                    if st.has(2):
                        act.wait_ge(product, st.count(back=2))
                    act.activation(hT[:, st.ring(2)], hT_ps[:, st.ring(2)], ACT.Copy).then_inc(hT_ready, 1)
                if st := slot.step(2):
                    if st.has(R):
                        act.wait_ge(turned, st.count(back=R))
                    norm.apply(act, st, h, x, ACT.Relu)

        @block.tensor
        def _(pe):
            for slot in slots(pe, steps, 5):
                if st := slot.step(5):
                    q = st.ring(2)
                    pe.wait_ge(hT_ready, st.count())
                    if st.has(2):
                        pe.wait_ge(y_ready, st.count(back=2))
                    for t in range(T):
                        last = pe.matmul(product_ps[:, q, t, :], hT[:, q, t, :], g["w_rel"][:, :], start=True, stop=True)
                    last.then_inc(product, 1)
                if st := slot.step(3):
                    pe.wait_ge(norm.normed, st.count())
                    if st.has(2):
                        pe.wait_ge(hT_ready, st.count(back=2))
                    for t in range(T):
                        last = pe.transpose(hT_ps[:, st.ring(2), t, :], h[:, st.ring(), t, :], g["ident"][:, :])
                    last.then_inc(turned, 1)


class EdgeSum:

    def __init__(self, s, name, g, C, tables, by, gather=None, load=None, weighted=False, first=False, extra=None):
        self.g, self.steps, self.tables, self.by = g, C // T, tables, by
        self.gather, self.load, self.weighted, self.first, self.extra = gather, load, weighted, first, extra
        self.W = P + {None: 0, "ones": 1, "exp": HEADS}[extra]
        self.adds = 16 * T // len(tables)
        self.moved = 16 * T if gather else 16
        self.scaled = weighted or extra == "exp"
        self.gather_idx = s.sb(name + "_gather_idx", [P, R, T], I32)
        self.target = s.sb(name + "_target", [P, R, T], I32)
        self.ids = s.sb(name + "_ids", [P, R, T])
        self.factor = s.sb(name + "_factor", [P, R, T])
        self.more = s.sb(name + "_more", [P, R, T, HEADS])
        self.messages = s.sb(name + "_messages", [P, R, T, P])
        self.same = s.sb(name + "_same", [P, R, T, P])
        self.earlier = s.sb(name + "_earlier", [P, 2, T, P])
        self.n_earlier, self.shift = s.sb(name + "_n_earlier", [P, 2, T]), s.sb(name + "_shift", [P, 2, T])
        self.totals = s.sb(name + "_totals", [P, R, T, self.W])
        self.id_rows = s.ps(name + "_id_rows", [P, 2, T, P])
        self.sums = s.ps(name + "_sums", [P, 2, T, 256 if extra else P])
        self.staged, self.gathered, self.scaled_ready = s.sem(name + "_staged"), s.sems(name + "_gathered"), s.sem(name + "_scaled_ready")
        self.id_rows_ready, self.same_ready = s.sem(name + "_id_rows_ready"), s.sem(name + "_same_ready")
        self.earlier_ready, self.counted = s.sem(name + "_earlier_ready"), s.sem(name + "_counted")
        self.shift_ready, self.target_ready = s.sem(name + "_shift_ready"), s.sem(name + "_target_ready")
        self.target_kept, self.summed, self.totals_ready = s.sem(name + "_target_kept"), s.sem(name + "_summed"), s.sem(name + "_totals_ready")
        self.added = [s.sem(f"{name}_added{k}") for k in range(len(tables))]

    def fetch(self, sp, slot):
        if self.load is not None and (st := slot.step(1)):
            r = st.ring()
            if st.has(R):
                sp.wait_ge(self.summed, st.count(back=R))
            sp.dma_start(self.messages[:, r], rows(self.load)[:, st.tiles(), :]).then_inc(self.gathered[r], 16)

    def stage(self, act, slot):
        g = self.g
        if st := slot.step(3):
            act.wait_ge(self.summed, st.count())
            if st.has(R):
                for k in range(len(self.tables)):
                    act.wait_ge(self.added[k], st.count(self.adds, back=R))
            act.activation(self.totals[:, st.ring()], self.sums[:, st.ring(2), :, 0:self.W], ACT.Copy
                           ).then_inc(self.totals_ready, 1)
        if self.weighted and (st := slot.step(2)):
            r = st.ring()
            act.wait_ge(self.gathered[r], st.landed(self.moved))
            for t in range(T):
                last = act.activation(self.messages[:, r, t, :], self.messages[:, r, t, :], ACT.Copy,
                                      scale=self.factor[:, r, t:t + 1])
            last.then_inc(self.scaled_ready, 1)
        if st := slot.step(0):
            r = st.ring()
            if st.has(R):
                act.wait_ge(self.summed, st.count(back=R))
                act.wait_ge(self.same_ready, st.count(back=R))
                if self.first:
                    act.wait_ge(self.target_ready, st.count(back=R))
                    act.wait_ge(self.target_kept, st.count(back=R))
                if self.scaled:
                    act.wait_ge(self.scaled_ready, st.count(back=R))
                if self.gather:
                    act.wait_ge(self.gathered[r], st.landed(self.moved, back=R))
                if not self.first:
                    for k in range(len(self.tables)):
                        act.wait_ge(self.added[k], st.count(self.adds, back=R))
            if self.gather:
                act.activation(self.gather_idx[:, r, :], self.gather[1][:, st.tiles()], ACT.Copy)
            if not self.first:
                act.activation(self.target[:, r, :], g[self.by + "_target"][:, st.tiles()], ACT.Copy)
            if self.weighted:
                act.activation(self.factor[:, r, :], g["weight"][:, st.tiles()], ACT.Copy)
            if self.extra == "exp":
                act.activation(self.more[:, r].rearrange("p t h -> p (t h)"), g["exps"][:, st.tiles(HEADS)], ACT.Copy)
            act.activation(self.ids[:, r, :], g[self.by + "_f"][:, st.tiles()], ACT.Copy).then_inc(self.staged, 1)

    def move(self, pool, slot, tiles):
        for t in tiles:
            if st := slot.step(4):
                r, k = st.ring(), t % len(self.tables)
                if t == 0:
                    pool.wait_ge(self.totals_ready, st.count())
                    pool.wait_ge(self.target_ready if self.first else self.staged, st.count())
                if t >= len(self.tables) or st.has(1):
                    pool.wait_ge(self.added[k], st.count(self.adds, back=1) + 16 * (t // len(self.tables)))
                apart(pool, st, self.g["passed"])
                pool.indirect_dma_start(
                    out=self.tables[k], out_offset=bass.IndirectOffsetOnAxis(self.target[:, r, t:t + 1], 0),
                    in_=self.totals[:, r, t, :], in_offset=None, compute_op=ALU.add,
                ).then_inc(self.added[k], 16)
            if self.gather and (st := slot.step(1)):
                r = st.ring()
                if t == 0:
                    if st.has(R):
                        pool.wait_ge(self.summed, st.count(back=R))
                    pool.wait_ge(self.staged, st.count())
                    apart(pool, st, self.g["passed"])
                pool.indirect_dma_start(
                    out=self.messages[:, r, t, :], out_offset=None, in_=self.gather[0],
                    in_offset=bass.IndirectOffsetOnAxis(self.gather_idx[:, r, t:t + 1], 0),
                ).then_inc(self.gathered[r], 16)

    def pace(self, eng, st, tile):
        if st.has(R):
            n = len(self.tables)
            eng.wait_ge(self.added[tile % n], st.count(self.adds, back=R + 1) + 16 * (tile // n + 1))

    def moved_all(self, pool):
        for k in range(len(self.tables)):
            pool.wait_ge(self.added[k], self.steps * self.adds)
        if self.gather:
            all_landed(pool, self.gathered, self.steps, self.moved)

    def multiply(self, pe, slot):
        if st := slot.step(3):
            r, q = st.ring(), st.ring(2)
            pe.wait_ge(self.same_ready, st.count())
            if self.scaled:
                pe.wait_ge(self.scaled_ready, st.count())
            else:
                pe.wait_ge(self.gathered[r], st.landed(self.moved))
            if st.has(2):
                pe.wait_ge(self.totals_ready, st.count(back=2))
            for t in range(T):
                last = pe.matmul(self.sums[:, q, t, 0:P], self.same[:, r, t, :], self.messages[:, r, t, :],
                                 start=True, stop=True)
                if self.extra:
                    cols = self.g["ones"][:, 0:1] if self.extra == "ones" else self.more[:, r, t, :]
                    last = pe.matmul(self.sums[:, q, t, P:self.W], self.same[:, r, t, :], cols, start=True, stop=True)
            last.then_inc(self.summed, 1)
        if st := slot.step(1):
            r, q = st.ring(), st.ring(2)
            pe.wait_ge(self.staged, st.count())
            if st.has(2):
                pe.wait_ge(self.same_ready, st.count(back=2))
            for t in range(T):
                last = pe.matmul(self.id_rows[:, q, t, :], self.ids[:, r, t:t + 1].to_broadcast([P, P]),
                                 self.g["ident"][:, :], start=True, stop=True)
            last.then_inc(self.id_rows_ready, 1)

    def compare(self, dve, slot):
        g = self.g
        if st := slot.step(2):
            r, q = st.ring(), st.ring(2)
            dve.wait_ge(self.id_rows_ready, st.count())
            if st.has(R):
                dve.wait_ge(self.summed, st.count(back=R))
            dve.tensor_tensor(self.same[:, r], self.id_rows[:, q],
                              self.ids[:, r].unsqueeze(2).to_broadcast([P, T, P]), ALU.is_equal).then_inc(self.same_ready, 1)
            if self.first:
                dve.wait_ge(self.same_ready, st.count())
                dve.tensor_tensor(self.earlier[:, q], self.same[:, r], over(g["before"]),
                                  ALU.mult).then_inc(self.earlier_ready, 1)
                dve.wait_ge(self.earlier_ready, st.count())
                dve.tensor_reduce(self.n_earlier[:, q, :], self.earlier[:, q], AX.X, ALU.add).then_inc(self.counted, 1)
                dve.wait_ge(self.counted, st.count())
                dve.scalar_tensor_tensor(out=self.shift[:, q, :], in0=self.n_earlier[:, q, :], scalar=1.0,
                                         in1=g[self.by + "_spare"][:, st.tiles()], op0=ALU.min, op1=ALU.mult
                                         ).then_inc(self.shift_ready, 1)
                dve.wait_ge(self.shift_ready, st.count())
                if st.has(R):
                    for k in range(len(self.tables)):
                        dve.wait_ge(self.added[k], st.count(self.adds, back=R))
                dve.tensor_tensor(self.target[:, r, :], self.shift[:, q, :], self.ids[:, r, :],
                                  ALU.add).then_inc(self.target_ready, 1)
                dve.tensor_tensor(g[self.by + "_target"][:, st.tiles()], self.shift[:, q, :], self.ids[:, r, :],
                                  ALU.add).then_inc(self.target_kept, 1)
            if self.extra == "exp":
                dve.wait_ge(self.gathered[r], st.landed(self.moved))
                view = self.messages[:, r].rearrange("p t (h d) -> p (t h) d", h=HEADS)
                factors = self.more[:, r].rearrange("p t h -> p (t h)").unsqueeze(2)
                dve.tensor_tensor(view, view, factors.to_broadcast([P, T * HEADS, P // HEADS]),
                                  ALU.mult).then_inc(self.scaled_ready, 1)

    def kept_all(self, dve):
        if self.first:
            dve.wait_ge(self.target_kept, self.steps)


def edge_sum(nc, g, C, name, tables, by, **kind):
    steps = C // T
    with ExitStack() as ctx:
        s = Scope(nc, ctx, name)
        edges = EdgeSum(s, "edges", g, C, tables, by, **kind)
        block = s.block()

        @block.sync
        def _(sp):
            if edges.load is not None:
                for slot in slots(sp, steps, 1):
                    edges.fetch(sp, slot)

        @block.scalar
        def _(act):
            for slot in slots(act, steps, 3):
                edges.stage(act, slot)

        @block.gpsimd
        def _(pool):
            for slot in slots(pool, steps, 4):
                edges.move(pool, slot, range(T))
            edges.moved_all(pool)

        @block.tensor
        def _(pe):
            for slot in slots(pe, steps, 3):
                edges.multiply(pe, slot)

        @block.vector
        def _(dve):
            for slot in slots(dve, steps, 2):
                edges.compare(dve, slot)
            edges.kept_all(dve)


def edge_sums(nc, g, C, zero):
    steps = C // T
    with ExitStack() as ctx:
        s = Scope(nc, ctx, "sums")
        rel = EdgeSum(s, "rel", g, C, g["agg_rel"], "src", gather=(g["y0"], g["dst_i"]), weighted=True, first=True)
        mlp = EdgeSum(s, "mlp", g, C, g["agg_mlp"], "dst", load=g["edge_attr_128"], first=True)
        zeroed = s.sem("zeroed")
        block = s.block()

        @block.sync
        def _(sp):
            zero_spare(sp, g, C, zero, zeroed)
            for slot in slots(sp, steps, 1):
                mlp.fetch(sp, slot)
                if st := slot.step(0):
                    zero_step(sp, g, C, zero, st, zeroed, beside=rel)
            sp.wait_ge(zeroed, zeroings(zero, steps))

        @block.scalar
        def _(act):
            for slot in slots(act, steps, 3):
                rel.stage(act, slot)
                mlp.stage(act, slot)

        @block.gpsimd
        def _(pool):
            for slot in slots(pool, steps, 4):
                for t in range(T):
                    rel.move(pool, slot, [t])
                    mlp.move(pool, slot, [t])
            rel.moved_all(pool)
            mlp.moved_all(pool)

        @block.tensor
        def _(pe):
            for slot in slots(pe, steps, 3):
                rel.multiply(pe, slot)
                mlp.multiply(pe, slot)

        @block.vector
        def _(dve):
            for slot in slots(dve, steps, 2):
                rel.compare(dve, slot)
                mlp.compare(dve, slot)
            rel.kept_all(dve)
            mlp.kept_all(dve)


def node_mlp(nc, g, C, zero):
    steps = C // T
    with ExitStack() as ctx:
        s = Scope(nc, ctx, "mlp")
        rel, x, x1, h, a, z, zn, xh, base, x2, h2 = (s.sb(k, [P, R, T, P]) for k in (
            "rel", "x", "x1", "h", "a", "z", "zn", "xh", "base", "x2", "h2"))
        inT = s.sb("inT", [P, 2, 2, T * P])
        hid = s.sb("hid", [P, 2, 2, T * P])
        hT_ps, aT_ps = s.ps("hT_ps", [P, T, P]), s.ps("aT_ps", [P, T, P])
        hid_ps, out_ps = s.ps("hid_ps", [P, 2, 2, T * P]), s.ps("out_ps", [P, 2, T, P])
        rel_landed, x_landed, a_landed = (s.sems(k + "_landed") for k in ("rel", "x", "a"))
        x2_stored, h2_stored = s.sems("x2_stored"), s.sems("h2_stored")
        x1_ready, xh_ready = s.sem("x1_ready"), s.sem("xh_ready")
        h_turned, a_turned, hT_ready, aT_ready, hid_product, hid_ready = (s.sem(k) for k in (
            "h_turned", "a_turned", "hT_ready", "aT_ready", "hid_product", "hid_ready"))
        out_product, z_ready, base_ready, gammaed, x2_ready = (s.sem(k) for k in (
            "out_product", "z_ready", "base_ready", "gammaed", "x2_ready"))
        norm0, norm1, norm2 = (Norm(s, k, g["minus_half"], g["passed"]) for k in ("ln0", "ln1", "ln2"))
        zeroed = s.sem("zeroed")
        block = s.block()

        @block.sync
        def _(sp):
            zero_spare(sp, g, C, zero, zeroed)
            for slot in slots(sp, steps, 13):
                if st := slot.step(13):
                    sp.wait_ge(norm2.normed, st.count())
                    sp.dma_start(rows(g["h2"])[:, st.tiles(), :], h2[:, st.ring()]).then_inc(h2_stored[st.ring()], 16)
                if st := slot.step(11):
                    sp.wait_ge(x2_ready, st.count())
                    sp.dma_start(rows(g["x2"])[:, st.tiles(), :], x2[:, st.ring()]).then_inc(x2_stored[st.ring()], 16)
                if st := slot.step(3):
                    if st.has(R):
                        sp.wait_ge(a_turned, st.count(back=R))
                    sp.dma_start(a[:, st.ring()], table_rows(g["agg_mlp"][0], C)[:, st.tiles(), :]
                                 ).then_inc(a_landed[st.ring()], 16)
                if st := slot.step(0):
                    r = st.ring()
                    if st.has(R):
                        sp.wait_ge(x1_ready, st.count(back=R))
                    sp.dma_start(rel[:, r], table_rows(g["agg_rel"][0], C)[:, st.tiles(), :]).then_inc(rel_landed[r], 16)
                    sp.dma_start(x[:, r], rows(g["x"])[:, st.tiles(), :]).then_inc(x_landed[r], 16)
                    zero_step(sp, g, C, zero, st, zeroed)
            for stored in (x2_stored, h2_stored):
                all_landed(sp, stored, steps, 16)
            sp.wait_ge(zeroed, zeroings(zero, steps))

        @block.vector
        def _(dve):
            for slot in slots(dve, steps, 12):
                if st := slot.step(10):
                    r = st.ring()
                    dve.wait_ge(norm1.normed, st.count())
                    dve.tensor_tensor(zn[:, r], zn[:, r], over(g["gamma_mlp"]), ALU.mult).then_inc(gammaed, 1)
                if st := slot.step(7):
                    r = st.ring()
                    dve.wait_ge(out_product, st.count())
                    if st.has(R):
                        dve.wait_ge(norm1.normed, st.count(back=R))
                    dve.tensor_tensor(z[:, r], out_ps[:, st.ring(2)], over(g["b2_mlp"]), ALU.add).then_inc(z_ready, 1)
                if st := slot.step(1):
                    r = st.ring()
                    dve.wait_ge(rel_landed[r], st.landed(16))
                    dve.wait_ge(x_landed[r], st.landed(16))
                    if st.has(R):
                        dve.wait_ge(norm0.normed, st.count(back=R))
                        dve.wait_ge(xh_ready, st.count(back=R))
                    dve.scalar_tensor_tensor(out=x1[:, r], in0=rel[:, r], scalar=0.0, in1=x[:, r],
                                             op0=ALU.max, op1=ALU.add).then_inc(x1_ready, 1)
                if st := slot.step(12):
                    norm2.shift(dve, st)
                if st := slot.step(9):
                    norm1.shift(dve, st)
                if st := slot.step(3):
                    norm0.shift(dve, st)
                if st := slot.step(10):
                    r = st.ring()
                    dve.wait_ge(gammaed, st.count())
                    dve.wait_ge(base_ready, st.count())
                    if st.has(R):
                        dve.wait_ge(x2_stored[r], st.landed(16, back=R))
                        dve.wait_ge(norm2.normed, st.count(back=R))
                    dve.tensor_tensor(x2[:, r], zn[:, r], base[:, r], ALU.add).then_inc(x2_ready, 1)
                if st := slot.step(7):
                    dve.wait_ge(z_ready, st.count())
                    norm1.statistics(dve, st, z)
                if st := slot.step(1):
                    dve.wait_ge(x1_ready, st.count())
                    norm0.statistics(dve, st, x1)
                if st := slot.step(7):
                    norm1.aggregate(dve, st)
                if st := slot.step(10):
                    dve.wait_ge(x2_ready, st.count())
                    norm2.statistics(dve, st, x2)
                if st := slot.step(1):
                    norm0.aggregate(dve, st)
                if st := slot.step(10):
                    norm2.aggregate(dve, st)

        @block.gpsimd
        def _(pool):
            for slot in slots(pool, steps, 11):
                if st := slot.step(7):
                    r = st.ring()
                    if st.has(R):
                        pool.wait_ge(x2_ready, st.count(back=R))
                    pool.wait_ge(xh_ready, st.count())
                    pool.tensor_tensor(base[:, r], xh[:, r], over(g["beta_mlp"]), ALU.add).then_inc(base_ready, 1)
                if st := slot.step(4):
                    r = st.ring()
                    pool.wait_ge(norm0.normed, st.count())
                    if st.has(R):
                        pool.wait_ge(base_ready, st.count(back=R))
                    pool.tensor_tensor(xh[:, r], x1[:, r], h[:, r], ALU.add).then_inc(xh_ready, 1)
                if st := slot.step(11):
                    norm2.power(pool, st)
                if st := slot.step(8):
                    norm1.power(pool, st)
                if st := slot.step(2):
                    norm0.power(pool, st)

        @block.scalar
        def _(act):
            for slot in slots(act, steps, 12):
                if st := slot.step(12):
                    if st.has(R):
                        act.wait_ge(h2_stored[st.ring()], st.landed(16, back=R))
                    norm2.apply(act, st, h2, x2, ACT.Relu)
                if st := slot.step(9):
                    if st.has(R):
                        act.wait_ge(x2_ready, st.count(back=R))
                    norm1.apply(act, st, zn, z, ACT.Identity)
                if st := slot.step(3):
                    if st.has(R):
                        act.wait_ge(h_turned, st.count(back=R))
                        act.wait_ge(xh_ready, st.count(back=R))
                    norm0.apply(act, st, h, x1, ACT.Relu)
                if st := slot.step(5):
                    act.wait_ge(hid_product, st.count())
                    if st.has(2):
                        act.wait_ge(out_product, st.count(back=2))
                    for m in range(2):
                        last = act.activation(hid[:, st.ring(2), m, :], hid_ps[:, st.ring(2), m, :], ACT.Silu,
                                              bias=g["b1_mlp"][:, m:m + 1])
                    last.then_inc(hid_ready, 1)
                if st := slot.step(4):
                    q = st.ring(2)
                    if st.has(2):
                        act.wait_ge(hid_product, st.count(back=2))
                    act.wait_ge(h_turned, st.count())
                    act.activation(inT[:, q, 0, :], hT_ps[:, :, :].rearrange("p t n -> p (t n)"), ACT.Copy).then_inc(hT_ready, 1)
                    act.wait_ge(a_turned, st.count())
                    act.activation(inT[:, q, 1, :], aT_ps[:, :, :].rearrange("p t n -> p (t n)"), ACT.Copy).then_inc(aT_ready, 1)

        @block.tensor
        def _(pe):
            for slot in slots(pe, steps, 6):
                if st := slot.step(6):
                    q = st.ring(2)
                    pe.wait_ge(hid_ready, st.count())
                    if st.has(2):
                        pe.wait_ge(z_ready, st.count(back=2))
                    for t in range(T):
                        for m in range(2):
                            last = pe.matmul(out_ps[:, q, t, :], hid[:, q, m, t * P:(t + 1) * P], g["w2_mlp"][:, m, :],
                                             start=(m == 0), stop=(m == 1))
                    last.then_inc(out_product, 1)
                if st := slot.step(5):
                    q = st.ring(2)
                    pe.wait_ge(hT_ready, st.count())
                    pe.wait_ge(aT_ready, st.count())
                    if st.has(2):
                        pe.wait_ge(hid_ready, st.count(back=2))
                    for m in range(2):
                        for k in range(2):
                            last = pe.matmul(hid_ps[:, q, m, :], g["w1_mlp"][:, k, m * P:(m + 1) * P], inT[:, q, k, :],
                                             start=(k == 0), stop=(k == 1))
                    last.then_inc(hid_product, 1)
                if st := slot.step(4):
                    r = st.ring()
                    pe.wait_ge(norm0.normed, st.count())
                    if st.has(1):
                        pe.wait_ge(hT_ready, st.count(back=1))
                    for t in range(T):
                        last = pe.transpose(hT_ps[:, t, :], h[:, r, t, :], g["ident"][:, :])
                    last.then_inc(h_turned, 1)
                    pe.wait_ge(a_landed[r], st.landed(16))
                    if st.has(1):
                        pe.wait_ge(aT_ready, st.count(back=1))
                    for t in range(T):
                        last = pe.transpose(aT_ps[:, t, :], a[:, r, t, :], g["ident"][:, :])
                    last.then_inc(a_turned, 1)


def edge_project(nc, g, C, zero):
    steps, D, EF = C // T, P, g["edge_attr_64"].shape[1]
    moved = 16 * T
    with ExitStack() as ctx:
        s = Scope(nc, ctx, "proj")
        idx = s.sb("idx", [P, R, T], I32)
        h, xp, weighed = s.sb("h", [P, R, T, D]), s.sb("xp", [P, R, T, D]), s.sb("weighed", [P, 2, T, D])
        attr, attrT, hT = s.sb("attr", [P, R, T, EF]), s.sb("attrT", [EF, 2, T, P]), s.sb("hT", [P, 2, T, P])
        attrT_ps, hT_ps, product_ps = s.ps("attrT_ps", [EF, 2, T, P]), s.ps("hT_ps", [P, 2, T, P]), s.ps("product_ps", [P, 2, T, D])
        staged, gathered, landed = s.sem("staged"), s.sems("gathered"), s.sems("landed")
        turned, attrT_ready, product = s.sem("turned"), s.sem("attrT_ready"), s.sem("product")
        h_turned, hT_ready = s.sem("h_turned"), s.sem("hT_ready")
        xp_ready, weighed_ready, scored, stored = s.sem("xp_ready"), s.sem("weighed_ready"), s.sem("scored"), s.sems("stored")
        zeroed = s.sem("zeroed")
        block = s.block()

        @block.sync
        def _(sp):
            zero_spare(sp, g, C, zero, zeroed)
            for slot in slots(sp, steps, 6):
                if st := slot.step(6):
                    sp.wait_ge(xp_ready, st.count())
                    sp.dma_start(rows(g["xp"])[:, st.tiles(), :], xp[:, st.ring()]).then_inc(stored[st.ring()], 16)
                if st := slot.step(0):
                    if st.has(R):
                        sp.wait_ge(turned, st.count(back=R))
                    sp.dma_start(attr[:, st.ring()], rows(g["edge_attr_64"])[:, st.tiles(), :]).then_inc(landed[st.ring()], 16)
                    zero_step(sp, g, C, zero, st, zeroed)
            all_landed(sp, stored, steps, 16)
            sp.wait_ge(zeroed, zeroings(zero, steps))

        @block.gpsimd
        def _(pool):
            for slot in slots(pool, steps, 1):
                if st := slot.step(1):
                    r = st.ring()
                    if st.has(R):
                        pool.wait_ge(h_turned, st.count(back=R))
                    pool.wait_ge(staged, st.count())
                    apart(pool, st, g["passed"])
                    for t in range(T):
                        pool.indirect_dma_start(
                            out=h[:, r, t, :], out_offset=None, in_=g["h2"],
                            in_offset=bass.IndirectOffsetOnAxis(idx[:, r, t:t + 1], 0)).then_inc(gathered[r], 16)
            all_landed(pool, gathered, steps, moved)

        @block.scalar
        def _(act):
            for slot in slots(act, steps, 3):
                if st := slot.step(3):
                    act.wait_ge(turned, st.count())
                    if st.has(2):
                        act.wait_ge(product, st.count(back=2))
                    act.activation(attrT[:, st.ring(2)], attrT_ps[:, st.ring(2)], ACT.Copy).then_inc(attrT_ready, 1)
                    act.wait_ge(h_turned, st.count())
                    act.activation(hT[:, st.ring(2)], hT_ps[:, st.ring(2)], ACT.Copy).then_inc(hT_ready, 1)
                if st := slot.step(0):
                    if st.has(R):
                        act.wait_ge(gathered[st.ring()], st.landed(moved, back=R))
                    act.activation(idx[:, st.ring(), :], g["src_i"][:, st.tiles()], ACT.Copy).then_inc(staged, 1)

        @block.tensor
        def _(pe):
            for slot in slots(pe, steps, 4):
                if st := slot.step(4):
                    q = st.ring(2)
                    pe.wait_ge(attrT_ready, st.count())
                    pe.wait_ge(hT_ready, st.count())
                    if st.has(2):
                        pe.wait_ge(xp_ready, st.count(back=2))
                    for t in range(T):
                        pe.matmul(product_ps[:, q, t, :], hT[:, q, t, :], g["w_node"][:, :], start=True, stop=False)
                        last = pe.matmul(product_ps[:, q, t, :], attrT[:, q, t, :], g["w_edge"][:, :], start=False, stop=True)
                    last.then_inc(product, 1)
                if st := slot.step(3):
                    if st.has(2):
                        pe.wait_ge(attrT_ready, st.count(back=2))
                        pe.wait_ge(hT_ready, st.count(back=2))
                    pe.wait_ge(landed[st.ring()], st.landed(16))
                    apart(pe, st, g["passed"])
                    for t in range(T):
                        last = pe.transpose(attrT_ps[:, st.ring(2), t, :], attr[:, st.ring(), t, :], g["ident"][:, :])
                    last.then_inc(turned, 1)
                    pe.wait_ge(gathered[st.ring()], st.landed(moved))
                    for t in range(T):
                        last = pe.transpose(hT_ps[:, st.ring(2), t, :], h[:, st.ring(), t, :], g["ident"][:, :])
                    last.then_inc(h_turned, 1)

        @block.vector
        def _(dve):
            for slot in slots(dve, steps, 5):
                if st := slot.step(5):
                    r, q = st.ring(), st.ring(2)
                    dve.wait_ge(product, st.count())
                    if st.has(R):
                        dve.wait_ge(stored[r], st.landed(16, back=R))
                    dve.tensor_tensor(xp[:, r], product_ps[:, q], over(g["b_proj"]), ALU.add).then_inc(xp_ready, 1)
                    dve.wait_ge(xp_ready, st.count())
                    dve.tensor_tensor(weighed[:, q], xp[:, r], over(g["attn"]), ALU.mult).then_inc(weighed_ready, 1)
                    dve.wait_ge(weighed_ready, st.count())
                    dve.tensor_reduce(g["scores"][:, st.tiles(HEADS)],
                                      weighed[:, q].rearrange("p t (h d) -> p (t h) d", h=HEADS), AX.X, ALU.add
                                      ).then_inc(scored, 1)
            dve.wait_ge(scored, steps)


def edge_exp_sorted(nc, g, C):
    H = HEADS
    with ExitStack() as ctx:
        s = Scope(nc, ctx, "sorted")
        link = s.sb("link", [P, C + 1])
        running, best = s.sb("running", [P, H, C]), s.sb("best", [P, H, C])
        ends = s.sb("ends", [P, 2])
        tails = s.sb("tails", [P, 2, H])
        carry = s.sb("carry", [P, H])
        ids, seam = s.sb("ids", [1, 2, P]), s.sb("seam", [1, P + 1])
        over_row = s.sb("over_row", [H, 2, P])
        row_scan, row_carry = s.sb("row_scan", [H, P]), s.sb("row_carry", [H, P])
        small = s.ps("small", [P, 512])
        dve_done, pe_done, act_done = s.sem("dve_done"), s.sem("pe_done"), s.sem("act_done")
        scores = g["scores"][:, :].rearrange("p (c h) -> p h c", h=H)
        exps = g["exps"][:, :].rearrange("p (c h) -> p h c", h=H)
        turns = []
        block = s.block()

        @block.vector
        def _(dve):
            n = [0]

            def then(instruction):
                n[0] += 1
                instruction.then_inc(dve_done, 1)
                dve.wait_ge(dve_done, n[0])

            def turned():
                turns.append(n[0])
                dve.wait_ge(pe_done, len(turns))

            dve.tensor_copy(ends[:, 0:1], g["dst_f"][:, 0:1])
            dve.memset(seam[:, :], -FAR)
            then(dve.tensor_copy(ends[:, 1:2], g["dst_f"][:, C - 1:C]))
            turned()
            then(dve.tensor_copy(ids[:, :, :], small[0:1, 0:2 * P].rearrange("o (k p) -> o k p", k=2)))
            then(dve.tensor_tensor(seam[:, 1:P], ids[:, 0, 1:P], ids[:, 1, 0:P - 1], ALU.not_equal))
            then(dve.tensor_scalar(seam[:, 1:P], seam[:, 1:P], -FAR, None, ALU.mult))
            turned()
            dve.tensor_copy(link[:, 0:1], small[:, 0:1])
            dve.tensor_copy(link[:, C:C + 1], small[:, 1:2])
            then(dve.tensor_tensor(link[:, 1:C], g["dst_f"][:, 1:C], g["dst_f"][:, 0:C - 1], ALU.not_equal))
            then(dve.tensor_scalar(link[:, 1:C], link[:, 1:C], -FAR, None, ALU.mult))
            for back in (False, True):
                order = slice(None, None, -1) if back else slice(None)
                links = link[:, 1:C + 1] if back else link[:, 0:C]
                source, result = (running, best) if back else (scores, running)
                for h in range(H):
                    last = dve.tensor_tensor_scan(result[:, h, :][:, order], links[:, order], source[:, h, :][:, order],
                                                  -FAR, ALU.add, ALU.max)
                then(last)
                then(dve.tensor_reduce(tails[:, 1, 0:1], links, AX.X, ALU.min))
                dve.tensor_copy(tails[:, 1, 1:H], tails[:, 1, 0:1].to_broadcast([P, H - 1]))
                end = 0 if back else C - 1
                then(dve.tensor_copy(tails[:, 0, :], result[:, :, end]))
                turned()
                then(dve.tensor_copy(over_row[:, :, :], small[0:H, 0:2 * P].rearrange("h (k p) -> h k p", k=2)))
                then(dve.tensor_tensor_scan(row_scan[:, order], over_row[:, 1, order], over_row[:, 0, order],
                                            -FAR, ALU.add, ALU.max))
                then(dve.memset(row_carry[:, :], -FAR))
                if back:
                    then(dve.tensor_copy(row_carry[:, 0:P - 1], row_scan[:, 1:P]))
                else:
                    then(dve.tensor_copy(row_carry[:, 1:P], row_scan[:, 0:P - 1]))
                turned()
                then(dve.tensor_copy(carry[:, :], small[:, 0:H]))
                for h in range(H):
                    last = dve.tensor_tensor_scan(result[:, h, :][:, order], links[:, order], source[:, h, :][:, order],
                                                  carry[:, h:h + 1], ALU.add, ALU.max)
                then(last)
            then(dve.tensor_tensor(exps, scores, best[:, :, :], ALU.subtract))
            turns.append(n[0])

        @block.tensor
        def _(pe):
            pe.wait_ge(dve_done, turns[0])
            for k in range(2):
                last = pe.transpose(small[0:1, k * P:(k + 1) * P], ends[:, k:k + 1], g["ident"][:, :])
            last.then_inc(pe_done, 1)
            pe.wait_ge(dve_done, turns[1])
            for k in range(2):
                last = pe.matmul(small[:, k:k + 1], seam[0:1, k:k + P], g["ones"][0:1, 0:1], start=True, stop=True)
            last.then_inc(pe_done, 1)
            for back in range(2):
                pe.wait_ge(dve_done, turns[2 + 2 * back])
                for k in range(2):
                    last = pe.transpose(small[0:H, k * P:(k + 1) * P], tails[:, k, :], g["ident"][:, :])
                last.then_inc(pe_done, 1)
                pe.wait_ge(dve_done, turns[3 + 2 * back])
                pe.transpose(small[:, 0:H], row_carry[:, :], g["ident"][0:H, 0:H]).then_inc(pe_done, 1)

        @block.scalar
        def _(act):
            act.wait_ge(dve_done, turns[6])
            act.activation(g["exps"][:, :], g["exps"][:, :], ACT.Exp).then_inc(act_done, 1)
            act.wait_ge(act_done, 1)


def edge_max(nc, g, C):
    steps, H = C // T, HEADS
    with ExitStack() as ctx:
        s = Scope(nc, ctx, "max")
        ids, target, own = s.sb("ids", [P, 2, T]), s.sb("target", [P, 2, T], I32), s.sb("own", [P, 2, T], I32)
        scores = s.sb("scores", [P, 2, T, H])
        away = s.sb("away", [P, 2, T, P])
        masked, best = s.sb("masked", [P, 2, T * H, P]), s.sb("best", [P, 2, T, H])
        seen, new = s.sb("seen", [P, 2, T, H]), s.sb("new", [P, 2, T, H])
        low, merged, lot = s.sb("low", [P, C * H]), s.sb("merged", [P, C * H]), s.sb("lot", [P, 2, C * H])
        id_rows, score_rows = s.ps("id_rows", [P, T, P]), s.ps("score_rows", [P, T * H, P])
        cleared, low_ready, staged, spread = s.sem("cleared"), s.sem("low_ready"), s.sem("staged"), s.sem("spread")
        same_ready, away_ready, masked_ready, best_ready = (s.sem(k) for k in (
            "same_ready", "away_ready", "masked_ready", "best_ready"))
        read, renewed, written = s.sem("read"), s.sem("renewed"), s.sem("written")
        lots, merging, final = s.sem("lots"), s.sem("merging"), s.sem("final")
        flat = [table_rows(m, C).rearrange("p c h -> p (c h)") for m in g["max_tables"]]
        block = s.block()

        @block.sync
        def _(sp):
            sp.wait_ge(low_ready, 1)
            for k, m in enumerate(g["max_tables"]):
                sp.dma_start(flat[k], low[:, :]).then_inc(cleared, 16)
                sp.dma_start(m[P * C:P * C + P, :], low[:, 0:H]).then_inc(cleared, 16)
            sp.wait_ge(cleared, 32 * T)
            sp.wait_ge(written, steps * 16 * T)
            sp.dma_start(merged[:, :], flat[0]).then_inc(lots, 16)
            for k in range(1, T):
                if k > 1:
                    sp.wait_ge(merging, k - 1)
                sp.dma_start(lot[:, k % 2, :], flat[k]).then_inc(lots, 16)
                sp.wait_ge(lots, 16 * (k + 1))
            sp.wait_ge(merging, T - 1)
            sp.dma_start(flat[0], merged[:, :]).then_inc(final, 16)
            sp.wait_ge(final, 16)

        @block.scalar
        def _(act):
            for slot in slots(act, steps, 0):
                if st := slot.step(0):
                    q = st.ring(2)
                    if st.has(2):
                        act.wait_ge(written, st.count(16 * T, back=2))
                    act.activation(ids[:, q, :], g["dst_f"][:, st.tiles()], ACT.Copy)
                    act.activation(target[:, q, :], g["dst_target"][:, st.tiles()], ACT.Copy)
                    act.activation(own[:, q, :], g["dst_i"][:, st.tiles()], ACT.Copy)
                    act.activation(scores[:, q].rearrange("p t h -> p (t h)"), g["scores"][:, st.tiles(H)],
                                   ACT.Copy).then_inc(staged, 1)

        @block.tensor
        def _(pe):
            for slot in slots(pe, steps, 1):
                if st := slot.step(1):
                    q = st.ring(2)
                    pe.wait_ge(staged, st.count())
                    if st.has(1):
                        pe.wait_ge(masked_ready, st.count(back=1))
                    for t in range(T):
                        pe.matmul(id_rows[:, t, :], ids[:, q, t:t + 1].to_broadcast([P, P]), g["ident"][:, :],
                                  start=True, stop=True)
                        for h in range(H):
                            last = pe.matmul(score_rows[:, t * H + h, :], scores[:, q, t, h:h + 1].to_broadcast([P, P]),
                                             g["ident"][:, :], start=True, stop=True)
                    last.then_inc(spread, 1)

        @block.vector
        def _(dve):
            dve.memset(low[:, :], -FAR).then_inc(low_ready, 1)
            for slot in slots(dve, steps, 3):
                if st := slot.step(3):
                    q = st.ring(2)
                    dve.wait_ge(read, st.count(16 * T))
                    dve.wait_ge(best_ready, st.count())
                    dve.tensor_tensor(new[:, q], seen[:, q], best[:, q], ALU.max).then_inc(renewed, 1)
                if st := slot.step(2):
                    q = st.ring(2)
                    dve.wait_ge(spread, st.count())
                    dve.tensor_tensor(away[:, q], id_rows[:, :, :], ids[:, q].unsqueeze(2).to_broadcast([P, T, P]),
                                      ALU.is_equal).then_inc(same_ready, 1)
                    dve.wait_ge(same_ready, st.count())
                    dve.tensor_scalar(away[:, q], away[:, q], -1.0, FAR, ALU.add, ALU.mult).then_inc(away_ready, 1)
                    dve.wait_ge(away_ready, st.count())
                    for t in range(T):
                        last = dve.tensor_tensor(masked[:, q, t * H:(t + 1) * H, :], score_rows[:, t * H:(t + 1) * H, :],
                                                 away[:, q, t, :].unsqueeze(1).to_broadcast([P, H, P]), ALU.add)
                    last.then_inc(masked_ready, 1)
                    dve.wait_ge(masked_ready, st.count())
                    dve.tensor_reduce(best[:, q].rearrange("p t h -> p (t h)"), masked[:, q], AX.X, ALU.max
                                      ).then_inc(best_ready, 1)
            for k in range(1, T):
                dve.wait_ge(lots, 16 * (k + 1))
                dve.tensor_tensor(merged[:, :], merged[:, :], lot[:, k % 2, :], ALU.max).then_inc(merging, 1)
                dve.wait_ge(merging, k)

        @block.gpsimd
        def _(pool):
            pool.wait_ge(cleared, 32 * T)
            for slot in slots(pool, steps, 3):
                if st := slot.step(3):
                    q = st.ring(2)
                    pool.wait_ge(staged, st.count())
                    if st.has(1):
                        pool.wait_ge(written, st.count(16 * T, back=1))
                    if st.has(2):
                        pool.wait_ge(renewed, st.count(back=2))
                    apart(pool, st, g["passed"])
                    for t in range(T):
                        pool.indirect_dma_start(
                            out=seen[:, q, t, :], out_offset=None, in_=g["max_tables"][t],
                            in_offset=bass.IndirectOffsetOnAxis(own[:, q, t:t + 1], 0)).then_inc(read, 16)
                    pool.wait_ge(renewed, st.count())
                    apart(pool, st, g["passed"])
                    for t in range(T):
                        pool.indirect_dma_start(
                            out=g["max_tables"][t], out_offset=bass.IndirectOffsetOnAxis(target[:, q, t:t + 1], 0),
                            in_=new[:, q, t, :], in_offset=None).then_inc(written, 16)
            pool.wait_ge(read, steps * 16 * T)
            pool.wait_ge(written, steps * 16 * T)


def edge_exp(nc, g, C):
    steps, H = C // T, HEADS
    moved = 16 * T
    with ExitStack() as ctx:
        s = Scope(nc, ctx, "exp")
        own, seen = s.sb("own", [P, R, T], I32), s.sb("seen", [P, R, T * H])
        staged, fetched, less, done = s.sem("staged"), s.sems("fetched"), s.sem("less"), s.sem("done")
        block = s.block()

        @block.gpsimd
        def _(pool):
            for slot in slots(pool, steps, 1):
                if st := slot.step(1):
                    r = st.ring()
                    if st.has(R):
                        pool.wait_ge(less, st.count(back=R))
                    pool.wait_ge(staged, st.count())
                    apart(pool, st, g["passed"])
                    for t in range(T):
                        pool.indirect_dma_start(
                            out=seen[:, r, t * H:(t + 1) * H], out_offset=None, in_=g["max_tables"][0],
                            in_offset=bass.IndirectOffsetOnAxis(own[:, r, t:t + 1], 0)).then_inc(fetched[r], 16)
            all_landed(pool, fetched, steps, moved)

        @block.vector
        def _(dve):
            for slot in slots(dve, steps, 2):
                if st := slot.step(2):
                    r = st.ring()
                    dve.wait_ge(fetched[r], st.landed(moved))
                    dve.tensor_tensor(g["exps"][:, st.tiles(H)], g["scores"][:, st.tiles(H)], seen[:, r, :],
                                      ALU.subtract).then_inc(less, 1)

        @block.scalar
        def _(act):
            for slot in slots(act, steps, 0):
                if st := slot.step(0):
                    if st.has(R):
                        act.wait_ge(fetched[st.ring()], st.landed(moved, back=R))
                    act.activation(own[:, st.ring(), :], g["dst_i"][:, st.tiles()], ACT.Copy).then_inc(staged, 1)
            act.wait_ge(less, steps)
            act.activation(g["exps"][:, :], g["exps"][:, :], ACT.Exp).then_inc(done, 1)
            act.wait_ge(done, 1)


def node_attn(nc, g, C):
    steps, H, W = C // T, HEADS, P + HEADS
    with ExitStack() as ctx:
        s = Scope(nc, ctx, "attn")
        a, b = s.sb("a", [P, R, T, W]), s.sb("b", [P, R, T, W])
        x, h, v, z, zn, base, x3, h3 = (s.sb(k, [P, R, T, P]) for k in ("x", "h", "v", "z", "zn", "base", "x3", "h3"))
        den, inv = s.sb("den", [P, 2, T, H]), s.sb("inv", [P, 2, T, H])
        vT = s.sb("vT", [P, 2, T, P])
        vT_ps, product_ps = s.ps("vT_ps", [P, 2, T, P]), s.ps("product_ps", [P, 2, T, P])
        a_landed, b_landed, x_landed, h_landed = (s.sems(k + "_landed") for k in "abxh")
        x3_stored, h3_stored = s.sems("x3_stored"), s.sems("h3_stored")
        agg_ready, den_ready, inv_ready, divided, v_ready, turned, vT_ready, product = (s.sem(k) for k in (
            "agg_ready", "den_ready", "inv_ready", "divided", "v_ready", "turned", "vT_ready", "product"))
        z_ready, gammaed, base_ready, x3_ready = (s.sem(k) for k in ("z_ready", "gammaed", "base_ready", "x3_ready"))
        norm1, norm2 = (Norm(s, k, g["minus_half"], g["passed"]) for k in ("ln1", "ln2"))
        tables = [table_rows(t, C) for t in g["agg_attn"]]
        block = s.block()

        @block.sync
        def _(sp):
            for slot in slots(sp, steps, 11):
                if st := slot.step(11):
                    sp.wait_ge(norm2.normed, st.count())
                    sp.dma_start(rows(g["h3"])[:, st.tiles(), :], h3[:, st.ring()]).then_inc(h3_stored[st.ring()], 16)
                if st := slot.step(9):
                    sp.wait_ge(x3_ready, st.count())
                    sp.dma_start(rows(g["x3"])[:, st.tiles(), :], x3[:, st.ring()]).then_inc(x3_stored[st.ring()], 16)
                if st := slot.step(5):
                    if st.has(R):
                        sp.wait_ge(base_ready, st.count(back=R))
                    sp.dma_start(x[:, st.ring()], rows(g["x2"])[:, st.tiles(), :]).then_inc(x_landed[st.ring()], 16)
                if st := slot.step(0):
                    r = st.ring()
                    if st.has(R):
                        sp.wait_ge(v_ready, st.count(back=R))
                    sp.dma_start(a[:, r], tables[0][:, st.tiles(), :]).then_inc(a_landed[r], 16)
                    sp.dma_start(b[:, r], tables[1][:, st.tiles(), :]).then_inc(b_landed[r], 16)
                    sp.dma_start(h[:, r], rows(g["h2"])[:, st.tiles(), :]).then_inc(h_landed[r], 16)
            for stored in (x3_stored, h3_stored):
                all_landed(sp, stored, steps, 16)

        @block.vector
        def _(dve):
            for slot in slots(dve, steps, 10):
                if st := slot.step(8):
                    r = st.ring()
                    dve.wait_ge(norm1.normed, st.count())
                    dve.tensor_tensor(zn[:, r], zn[:, r], over(g["gamma_attn"]), ALU.mult).then_inc(gammaed, 1)
                if st := slot.step(5):
                    dve.wait_ge(z_ready, st.count())
                    norm1.statistics(dve, st, z)
                if st := slot.step(10):
                    norm2.shift(dve, st)
                if st := slot.step(7):
                    norm1.shift(dve, st)
                if st := slot.step(8):
                    r = st.ring()
                    dve.wait_ge(gammaed, st.count())
                    dve.wait_ge(base_ready, st.count())
                    if st.has(R):
                        dve.wait_ge(x3_stored[r], st.landed(16, back=R))
                        dve.wait_ge(norm2.normed, st.count(back=R))
                    dve.tensor_tensor(x3[:, r], zn[:, r], base[:, r], ALU.add).then_inc(x3_ready, 1)
                if st := slot.step(1):
                    r = st.ring()
                    dve.wait_ge(a_landed[r], st.landed(16))
                    dve.wait_ge(b_landed[r], st.landed(16))
                    if st.has(R):
                        dve.wait_ge(turned, st.count(back=R))
                    dve.tensor_tensor(den[:, st.ring(2)], a[:, r, :, P:W], b[:, r, :, P:W], ALU.add)
                    dve.tensor_tensor(v[:, r], a[:, r, :, 0:P], b[:, r, :, 0:P], ALU.add).then_inc(agg_ready, 1)
                if st := slot.step(8):
                    dve.wait_ge(x3_ready, st.count())
                    norm2.statistics(dve, st, x3)
                if st := slot.step(1):
                    dve.wait_ge(agg_ready, st.count())
                    dve.tensor_scalar(den[:, st.ring(2)], den[:, st.ring(2)], 1.0, None, ALU.max).then_inc(den_ready, 1)
                if st := slot.step(5):
                    norm1.aggregate(dve, st)
                if st := slot.step(1):
                    dve.wait_ge(den_ready, st.count())
                    dve.reciprocal(inv[:, st.ring(2)], den[:, st.ring(2)]).then_inc(inv_ready, 1)
                if st := slot.step(8):
                    norm2.aggregate(dve, st)
                if st := slot.step(1):
                    r, q = st.ring(), st.ring(2)
                    dve.wait_ge(inv_ready, st.count())
                    view = v[:, r].rearrange("p t (h d) -> p (t h) d", h=H)
                    factors = inv[:, q].rearrange("p t h -> p (t h)").unsqueeze(2)
                    dve.tensor_tensor(view, view, factors.to_broadcast([P, T * H, P // H]), ALU.mult).then_inc(divided, 1)

        @block.gpsimd
        def _(pool):
            for slot in slots(pool, steps, 9):
                if st := slot.step(2):
                    r = st.ring()
                    pool.wait_ge(h_landed[r], st.landed(16))
                    pool.wait_ge(divided, st.count())
                    pool.tensor_tensor(v[:, r], v[:, r], h[:, r], ALU.add).then_inc(v_ready, 1)
                if st := slot.step(7):
                    r = st.ring()
                    if st.has(R):
                        pool.wait_ge(x3_ready, st.count(back=R))
                    pool.wait_ge(x_landed[r], st.landed(16))
                    pool.tensor_tensor(base[:, r], x[:, r], over(g["beta_attn"]), ALU.add).then_inc(base_ready, 1)
                if st := slot.step(9):
                    norm2.power(pool, st)
                if st := slot.step(6):
                    norm1.power(pool, st)

        @block.scalar
        def _(act):
            for slot in slots(act, steps, 10):
                if st := slot.step(10):
                    if st.has(R):
                        act.wait_ge(h3_stored[st.ring()], st.landed(16, back=R))
                    norm2.apply(act, st, h3, x3, ACT.Relu)
                if st := slot.step(7):
                    if st.has(R):
                        act.wait_ge(x3_ready, st.count(back=R))
                    norm1.apply(act, st, zn, z, ACT.Identity)
                if st := slot.step(4):
                    act.wait_ge(product, st.count())
                    if st.has(R):
                        act.wait_ge(norm1.normed, st.count(back=R))
                    act.activation(z[:, st.ring()], product_ps[:, st.ring(2)], ACT.Relu).then_inc(z_ready, 1)
                if st := slot.step(2):
                    act.wait_ge(turned, st.count())
                    if st.has(2):
                        act.wait_ge(product, st.count(back=2))
                    act.activation(vT[:, st.ring(2)], vT_ps[:, st.ring(2)], ACT.Copy).then_inc(vT_ready, 1)

        @block.tensor
        def _(pe):
            for slot in slots(pe, steps, 3):
                if st := slot.step(3):
                    q = st.ring(2)
                    pe.wait_ge(vT_ready, st.count())
                    if st.has(2):
                        pe.wait_ge(z_ready, st.count(back=2))
                    for t in range(T):
                        pe.matmul(product_ps[:, q, t, :], g["ones_row"][:, :], g["b_out"][0:1, :], start=True, stop=False)
                        last = pe.matmul(product_ps[:, q, t, :], vT[:, q, t, :], g["w_out"][:, :], start=False, stop=True)
                    last.then_inc(product, 1)
                if st := slot.step(2):
                    pe.wait_ge(v_ready, st.count())
                    if st.has(2):
                        pe.wait_ge(vT_ready, st.count(back=2))
                    for t in range(T):
                        last = pe.transpose(vT_ps[:, st.ring(2), t, :], v[:, st.ring(), t, :], g["ident"][:, :])
                    last.then_inc(turned, 1)


def node_sage(nc, g, C):
    steps, W = C // T, P + 1
    with ExitStack() as ctx:
        s = Scope(nc, ctx, "sage")
        a, b = s.sb("a", [P, R, T, W]), s.sb("b", [P, R, T, W])
        h, mean, g4 = (s.sb(k, [P, R, T, P]) for k in ("h", "mean", "g4"))
        inT = s.sb("inT", [P, 2, 2, T * P])
        hid = s.sb("hid", [P, R, 2, T * P])
        count, inv = s.sb("count", [P, 2, T]), s.sb("inv", [P, 2, T])
        mT_ps, hT_ps = s.ps("mT_ps", [P, T, P]), s.ps("hT_ps", [P, T, P])
        hid_ps, g4_ps = s.ps("hid_ps", [P, 2, 2, T * P]), s.ps("g4_ps", [P, 2, T, P])
        a_landed, b_landed, h_landed = (s.sems(k + "_landed") for k in "abh")
        g4_stored, hid_stored = s.sems("g4_stored"), s.sems("hid_stored")
        agg_ready, count_ready, inv_ready, mean_ready, m_turned, h_turned, mT_ready, hT_ready = (s.sem(k) for k in (
            "agg_ready", "count_ready", "inv_ready", "mean_ready", "m_turned", "h_turned", "mT_ready", "hT_ready"))
        hid_product, hid_ready, out_product, g4_ready = (s.sem(k) for k in (
            "hid_product", "hid_ready", "out_product", "g4_ready"))
        tables = [table_rows(t, C) for t in g["agg_sage1"]]
        block = s.block()

        @block.sync
        def _(sp):
            for slot in slots(sp, steps, 6):
                if st := slot.step(6):
                    r = st.ring()
                    sp.wait_ge(g4_ready, st.count())
                    sp.dma_start(rows(g["g4"])[:, st.tiles(), :], g4[:, r]).then_inc(g4_stored[r], 16)
                if st := slot.step(4):
                    r = st.ring()
                    sp.wait_ge(hid_ready, st.count())
                    sp.dma_start(hidden(g["h4T"], st), hid[:, r].rearrange("p m n -> p (m n)")).then_inc(hid_stored[r], 16)
                if st := slot.step(0):
                    r = st.ring()
                    if st.has(R):
                        sp.wait_ge(mean_ready, st.count(back=R))
                        sp.wait_ge(h_turned, st.count(back=R))
                    sp.dma_start(a[:, r], tables[0][:, st.tiles(), :]).then_inc(a_landed[r], 16)
                    sp.dma_start(b[:, r], tables[1][:, st.tiles(), :]).then_inc(b_landed[r], 16)
                    sp.dma_start(h[:, r], rows(g["h3"])[:, st.tiles(), :]).then_inc(h_landed[r], 16)
            for stored in (g4_stored, hid_stored):
                all_landed(sp, stored, steps, 16)

        @block.vector
        def _(dve):
            for slot in slots(dve, steps, 1):
                if st := slot.step(1):
                    r, q = st.ring(), st.ring(2)
                    dve.wait_ge(a_landed[r], st.landed(16))
                    dve.wait_ge(b_landed[r], st.landed(16))
                    dve.tensor_tensor(a[:, r], a[:, r], b[:, r], ALU.add).then_inc(agg_ready, 1)
                    dve.wait_ge(agg_ready, st.count())
                    dve.tensor_scalar(count[:, q, :], a[:, r, :, P], 1.0, None, ALU.max).then_inc(count_ready, 1)
                    dve.wait_ge(count_ready, st.count())
                    dve.reciprocal(g["inv_count"][:, st.tiles()], count[:, q, :])
                    dve.reciprocal(inv[:, q, :], count[:, q, :]).then_inc(inv_ready, 1)
                    dve.wait_ge(inv_ready, st.count())
                    if st.has(R):
                        dve.wait_ge(m_turned, st.count(back=R))
                    dve.tensor_tensor(mean[:, r], a[:, r, :, 0:P], inv[:, q, :].unsqueeze(2).to_broadcast([P, T, P]),
                                      ALU.mult).then_inc(mean_ready, 1)

        @block.scalar
        def _(act):
            for slot in slots(act, steps, 5):
                if st := slot.step(5):
                    r = st.ring()
                    act.wait_ge(out_product, st.count())
                    if st.has(R):
                        act.wait_ge(g4_stored[r], st.landed(16, back=R))
                    act.activation(g4[:, r], g4_ps[:, st.ring(2)], ACT.Copy).then_inc(g4_ready, 1)
                if st := slot.step(3):
                    act.wait_ge(hid_product, st.count())
                    if st.has(R):
                        act.wait_ge(out_product, st.count(back=R))
                        act.wait_ge(hid_stored[st.ring()], st.landed(16, back=R))
                    for m in range(2):
                        last = act.activation(hid[:, st.ring(), m, :], hid_ps[:, st.ring(2), m, :], ACT.Relu,
                                              bias=g["b1_sage"][:, m:m + 1])
                    last.then_inc(hid_ready, 1)
                if st := slot.step(2):
                    q = st.ring(2)
                    if st.has(2):
                        act.wait_ge(hid_product, st.count(back=2))
                    act.wait_ge(h_turned, st.count())
                    act.activation(inT[:, q, 1, :], hT_ps[:, :, :].rearrange("p t n -> p (t n)"), ACT.Copy).then_inc(hT_ready, 1)
                    act.wait_ge(m_turned, st.count())
                    act.activation(inT[:, q, 0, :], mT_ps[:, :, :].rearrange("p t n -> p (t n)"), ACT.Copy).then_inc(mT_ready, 1)

        @block.tensor
        def _(pe):
            for slot in slots(pe, steps, 5):
                if st := slot.step(5):
                    q = st.ring(2)
                    pe.wait_ge(hid_ready, st.count())
                    if st.has(2):
                        pe.wait_ge(g4_ready, st.count(back=2))
                    for t in range(T):
                        for m in range(2):
                            last = pe.matmul(g4_ps[:, q, t, :], hid[:, st.ring(), m, t * P:(t + 1) * P],
                                             g["w2_sage"][:, m, 0:P], start=(m == 0), stop=(m == 1))
                    last.then_inc(out_product, 1)
                if st := slot.step(3):
                    q = st.ring(2)
                    pe.wait_ge(mT_ready, st.count())
                    pe.wait_ge(hT_ready, st.count())
                    if st.has(2):
                        pe.wait_ge(hid_ready, st.count(back=2))
                    for m in range(2):
                        for k in range(2):
                            last = pe.matmul(hid_ps[:, q, m, :], g["w1_sage"][:, k, m * P:(m + 1) * P], inT[:, q, k, :],
                                             start=(k == 0), stop=(k == 1))
                    last.then_inc(hid_product, 1)
                if st := slot.step(2):
                    r = st.ring()
                    pe.wait_ge(h_landed[r], st.landed(16))
                    if st.has(1):
                        pe.wait_ge(hT_ready, st.count(back=1))
                    for t in range(T):
                        last = pe.transpose(hT_ps[:, t, :], h[:, r, t, :], g["ident"][:, :])
                    last.then_inc(h_turned, 1)
                    pe.wait_ge(mean_ready, st.count())
                    if st.has(1):
                        pe.wait_ge(mT_ready, st.count(back=1))
                    for t in range(T):
                        last = pe.transpose(mT_ps[:, t, :], mean[:, r, t, :], g["ident"][:, :])
                    last.then_inc(m_turned, 1)


def edge_sum_and_root(nc, g, C):
    steps = C // T
    with ExitStack() as ctx:
        s = Scope(nc, ctx, "root")
        edges = EdgeSum(s, "edges", g, C, g["agg_sage2"], "dst", gather=(g["g4"], g["src_i"]))
        hid, x, r4 = s.sb("hid", [P, R, 2, T * P]), s.sb("x", [P, R, T, P]), s.sb("r4", [P, R, T, P])
        r4_ps = s.ps("r4_ps", [P, 2, T, P])
        hid_landed, x_landed, r4_stored = s.sems("hid_landed"), s.sems("x_landed"), s.sems("r4_stored")
        base_ready, product, r4_ready = s.sem("base_ready"), s.sem("product"), s.sem("r4_ready")
        block = s.block()

        @block.sync
        def _(sp):
            for slot in slots(sp, steps, 4):
                if st := slot.step(0):
                    r = st.ring()
                    if st.has(R):
                        sp.wait_ge(product, st.count(back=R))
                    sp.dma_start(hid[:, r].rearrange("p m n -> p (m n)"), hidden(g["h4T"], st)).then_inc(hid_landed[r], 16)
                    edges.pace(sp, st, 0)
                    if st.has(R):
                        sp.wait_ge(base_ready, st.count(back=R))
                    sp.dma_start(x[:, r], rows(g["x3"])[:, st.tiles(), :]).then_inc(x_landed[r], 16)
                    edges.pace(sp, st, 2)
                if st := slot.step(4):
                    sp.wait_ge(r4_ready, st.count())
                    sp.dma_start(rows(g["r4"])[:, st.tiles(), :], r4[:, st.ring()]).then_inc(r4_stored[st.ring()], 16)
            all_landed(sp, r4_stored, steps, 16)

        @block.scalar
        def _(act):
            for slot in slots(act, steps, 3):
                edges.stage(act, slot)

        @block.gpsimd
        def _(pool):
            for slot in slots(pool, steps, 4):
                edges.move(pool, slot, range(T))
            edges.moved_all(pool)

        @block.tensor
        def _(pe):
            for slot in slots(pe, steps, 3):
                edges.multiply(pe, slot)
                if st := slot.step(2):
                    q = st.ring(2)
                    pe.wait_ge(hid_landed[st.ring()], st.landed(16))
                    if st.has(2):
                        pe.wait_ge(r4_ready, st.count(back=2))
                    for t in range(T):
                        for m in range(2):
                            last = pe.matmul(r4_ps[:, q, t, :], hid[:, st.ring(), m, t * P:(t + 1) * P],
                                             g["w2_sage"][:, m, P:2 * P], start=(m == 0), stop=(m == 1))
                    last.then_inc(product, 1)

        @block.vector
        def _(dve):
            for slot in slots(dve, steps, 3):
                edges.compare(dve, slot)
                if st := slot.step(3):
                    r = st.ring()
                    dve.wait_ge(base_ready, st.count())
                    dve.wait_ge(product, st.count())
                    dve.tensor_tensor(r4[:, r], r4[:, r], r4_ps[:, st.ring(2)], ALU.add).then_inc(r4_ready, 1)
                if st := slot.step(2):
                    r = st.ring()
                    dve.wait_ge(x_landed[r], st.landed(16))
                    if st.has(R):
                        dve.wait_ge(r4_stored[r], st.landed(16, back=R))
                    dve.tensor_tensor(r4[:, r], x[:, r], over(g["b2_sage"]), ALU.add).then_inc(base_ready, 1)


def node_out(nc, g, C):
    steps = C // T
    with ExitStack() as ctx:
        s = Scope(nc, ctx, "out")
        a, b, x, y = (s.sb(k, [P, R, T, P]) for k in ("a", "b", "x", "y"))
        inv = s.sb("inv", [P, R, T])
        a_landed, b_landed, x_landed = (s.sems(k + "_landed") for k in "abx")
        staged, agg_ready, scaled, y_ready, y_stored = (
            s.sem("staged"), s.sem("agg_ready"), s.sem("scaled"), s.sem("y_ready"), s.sems("y_stored"))
        tables = [table_rows(t, C) for t in g["agg_sage2"]]
        block = s.block()

        @block.sync
        def _(sp):
            for slot in slots(sp, steps, 3):
                if st := slot.step(3):
                    r = st.ring()
                    sp.wait_ge(y_ready, st.count())
                    sp.dma_start(rows(g["out"])[:, st.tiles(), :], y[:, r]).then_inc(y_stored[r], 16)
                if st := slot.step(0):
                    r = st.ring()
                    if st.has(R):
                        sp.wait_ge(y_ready, st.count(back=R))
                    sp.dma_start(a[:, r], tables[0][:, st.tiles(), :]).then_inc(a_landed[r], 16)
                    sp.dma_start(b[:, r], tables[1][:, st.tiles(), :]).then_inc(b_landed[r], 16)
                    sp.dma_start(x[:, r], rows(g["r4"])[:, st.tiles(), :]).then_inc(x_landed[r], 16)
            all_landed(sp, y_stored, steps, 16)

        @block.vector
        def _(dve):
            for slot in slots(dve, steps, 2):
                if st := slot.step(2):
                    r = st.ring()
                    dve.wait_ge(scaled, st.count())
                    dve.wait_ge(x_landed[r], st.landed(16))
                    dve.tensor_tensor(y[:, r], y[:, r], x[:, r], ALU.add).then_inc(y_ready, 1)
                if st := slot.step(1):
                    r = st.ring()
                    dve.wait_ge(a_landed[r], st.landed(16))
                    dve.wait_ge(b_landed[r], st.landed(16))
                    dve.tensor_tensor(a[:, r], a[:, r], b[:, r], ALU.add).then_inc(agg_ready, 1)

        @block.scalar
        def _(act):
            for slot in slots(act, steps, 1):
                if st := slot.step(1):
                    r = st.ring()
                    act.wait_ge(staged, st.count())
                    act.wait_ge(agg_ready, st.count())
                    if st.has(R):
                        act.wait_ge(y_stored[r], st.landed(16, back=R))
                    for t in range(T):
                        last = act.activation(y[:, r, t, :], a[:, r, t, :], ACT.Copy, scale=inv[:, r, t:t + 1])
                    last.then_inc(scaled, 1)
                if st := slot.step(0):
                    r = st.ring()
                    if st.has(R):
                        act.wait_ge(scaled, st.count(back=R))
                    act.activation(inv[:, r, :], g["inv_count"][:, st.tiles()], ACT.Copy).then_inc(staged, 1)


def build(nc, g, C):
    N = P * C
    with ExitStack() as ctx:
        def sb(name, shape, dt=F32):
            g[name] = ctx.enter_context(nc.sbuf_tensor(name, shape, dt))
            return g[name]

        def dram(name, shape):
            return nc.dram_tensor(name, shape, F32, kind="Internal").ap()

        for name in ("y0", "x2", "h2", "xp", "x3", "h3", "g4", "r4"):
            g[name] = dram("rows_" + name, (N, P))
        g["h4T"] = dram("h4T", (P, C * 2 * P))
        for name, width, copies in (("rel", P, 1), ("mlp", P, 1), ("attn", P + HEADS, TABLES),
                                    ("sage1", P + 1, TABLES), ("sage2", P, TABLES)):
            g["agg_" + name] = [dram(f"agg_{name}{k}", (N + P, width)) for k in range(copies)]
        g["max_tables"] = [dram(f"maxima{t}", (N + P, HEADS)) for t in range(T)]

        for key in ("src", "dst"):
            sb(key + "_i", [P, C], I32)
            for form in ("_f", "_spare", "_target"):
                sb(key + form, [P, C])
        sb("weight", [P, C])
        sb("scores", [P, C * HEADS])
        sb("exps", [P, C * HEADS])
        sb("inv_count", [P, C])
        sb("ident", [P, P])
        sb("before", [P, P])
        sb("ones", [P, 1])
        sb("ones_row", [1, P])
        sb("minus_half", [P, T])
        sb("spare_i", [P, 1], I32)
        sb("spare_f", [P, 1])
        sb("zeros", [P, T * (P + HEADS)])
        sb("unsorted_i", [P, 1], I32)
        g["unsorted"] = nc.dram_tensor("unsorted", (1, 1), I32, kind="Internal").ap()
        loads = []

        def const(name, shape, dram_ap):
            sb(name, shape)
            loads.append((g[name][:], dram_ap))

        const("w_rel", [P, P], g["L0_w"])
        const("w1_mlp", [P, 2, 2 * P], g["L1_gnn_W1"].rearrange("(k p) n -> p k n", p=P))
        const("w2_mlp", [P, 2, P], g["L1_gnn_W2"].rearrange("(k p) n -> p k n", p=P))
        const("b1_mlp", [P, 2], g["L1_b1"])
        E = g["edge_attr_64"].shape[1]
        const("w_node", [P, P], g["L2_w_proj"][0:P, :])
        const("w_edge", [E, P], g["L2_w_proj"][P:P + E, :])
        const("w_out", [P, P], g["L2_w_out"])
        sb("w1_sage", [P, 2, 2 * P])
        sb("w2_sage", [P, 2, 2 * P])
        for k, half in enumerate(("l", "r")):
            loads.append((g["w1_sage"][:, k, :], g["L3_gnn_W1_" + half]))
            loads.append((g["w2_sage"][:, :, k * P:(k + 1) * P], g["L3_gnn_W2_" + half].rearrange("(k p) n -> p k n", p=P)))
        const("b1_sage", [P, 2], g["L3_b1"])
        for name, key in (("b2_mlp", "L1_gnn_b2"), ("gamma_mlp", "L1_gnn_ln_gamma"), ("beta_mlp", "L1_gnn_ln_beta"),
                          ("b_proj", "L2_gnn_W_proj_b"), ("attn", "L2_attn"), ("b_out", "L2_gnn_W_out_b"),
                          ("gamma_attn", "L2_gnn_ln_gamma"), ("beta_attn", "L2_gnn_ln_beta"), ("b2_sage", "L3_gnn_b2")):
            const(name, [P, P], g[key].rearrange("(o n) -> o n", o=1).to_broadcast([P, P]))
        g["loads"] = loads

        g["passed"] = ctx.enter_context(nc.semaphore("passed"))
        setup(nc, g, C)
        node_norm(nc, g, C, zero=g["agg_rel"] + g["agg_mlp"])
        edge_sums(nc, g, C, zero=g["agg_attn"])
        node_mlp(nc, g, C, zero=g["agg_sage2"])
        edge_project(nc, g, C, zero=g["agg_sage1"])
        unsorted = nc.values_load(g["unsorted"])
        with nc.If(unsorted == 0):
            edge_exp_sorted(nc, g, C)
        with nc.Else():
            edge_max(nc, g, C)
            edge_exp(nc, g, C)
        edge_sum(nc, g, C, "attn_sum", g["agg_attn"], "dst", load=g["xp"], extra="exp")
        node_attn(nc, g, C)
        edge_sum(nc, g, C, "sage1_sum", g["agg_sage1"], "dst", gather=(g["h3"], g["src_i"]), extra="ones")
        node_sage(nc, g, C)
        edge_sum_and_root(nc, g, C)
        node_out(nc, g, C)


def kernel(**inputs):
    import concourse.bacc as bacc
    from concourse.bass_utils import run_bass_kernel_spmd

    nodes, D = inputs["x"].shape
    edges = inputs["src"].shape[0]
    C = -(-(max(nodes, edges) + 1) // (P * T)) * T

    def padded(a, value=0):
        a = np.asarray(a)
        return np.concatenate([a, np.full((P * C - a.shape[0],) + a.shape[1:], value, a.dtype)])

    halves = lambda b: np.ascontiguousarray(np.asarray(b).reshape(2, P).T)
    arrays = {
        "x": padded(inputs["x"]),
        "src": padded(inputs["src"], nodes),
        "dst": padded(inputs["dst"], nodes),
        "edge_weight": padded(inputs["edge_weight"]),
        "edge_attr_128": padded(inputs["edge_attr_128"]),
        "edge_attr_64": padded(inputs["edge_attr_64"]),
        "L0_w": np.ascontiguousarray(np.asarray(inputs["L0_gnn_weights"])[0].T),
        "L1_b1": halves(inputs["L1_gnn_b1"]),
        "L2_w_proj": np.ascontiguousarray(np.asarray(inputs["L2_gnn_W_proj_w"]).T),
        "L2_w_out": np.ascontiguousarray(np.asarray(inputs["L2_gnn_W_out_w"]).T),
        "L2_attn": np.asarray(inputs["L2_gnn_attn_vec"]).reshape(-1),
        "L3_b1": halves(inputs["L3_gnn_b1"]),
    }
    for name in ("L1_gnn_W1", "L1_gnn_W2", "L1_gnn_b2", "L1_gnn_ln_gamma", "L1_gnn_ln_beta", "L2_gnn_W_proj_b",
                 "L2_gnn_W_out_b", "L2_gnn_ln_gamma", "L2_gnn_ln_beta", "L3_gnn_W1_l", "L3_gnn_W1_r",
                 "L3_gnn_W2_l", "L3_gnn_W2_r", "L3_gnn_b2"):
        arrays[name] = np.ascontiguousarray(inputs[name])
    nc = bacc.Bacc("TRN2", target_bir_lowering=False, num_devices=1)
    g = {name: nc.dram_tensor(name, a.shape, mybir.dt.from_np(a.dtype), kind="ExternalInput").ap()
         for name, a in arrays.items()}
    g["out"] = nc.dram_tensor("out", (P * C, D), F32, kind="ExternalOutput").ap()
    build(nc, g, C)
    result = run_bass_kernel_spmd(nc, [arrays], core_ids=[0])
    return result.results[0]["out"][:nodes]
```
